# Optimizing a Trainium2 kernel written in Bass

```python
import numpy as np
import jax
import jax.numpy as jnp

def _softmax(x, axis=-1):
    return jax.nn.softmax(x, axis=axis)

def _gelu(x):
    return jax.nn.gelu(x, approximate=True)

def _silu(x):
    return jax.nn.silu(x)

def _sigmoid(x):
    return jax.nn.sigmoid(x)

def _layernorm(x, axis=-1, eps=1e-05):
    m = jnp.mean(x, axis=axis, keepdims=True)
    v = jnp.var(x, axis=axis, keepdims=True)
    return (x - m) / jnp.sqrt(v + eps)

def _scatter_add(tgt, idx, src, axis=0):
    return tgt.at[idx].add(src)

def _segment_sum(src, seg, n):
    return jax.ops.segment_sum(src, seg, n)
kernel_name = 'mk_gnn_preln_d2_gnn_r8_c8a63d'

def setup_inputs(seed: int=0):
    np.random.seed(seed)
    _w = jnp.asarray

    def _rec_inputs():
        import jax
        import jax.numpy as jnp
        _gk = jax.random.key(seed)
        x = -0.0003713 + 1 * jax.random.normal(jax.random.fold_in(_gk, 1), (12500, 128), jnp.float32)
        src = jax.random.randint(jax.random.fold_in(_gk, 2), (400000,), 0, 12500, jnp.int32)
        dst = jnp.minimum((12500 * jax.random.uniform(jax.random.fold_in(_gk, 3), (400000,)) ** 2.0).astype(jnp.int32), 99999)
        _o = jnp.argsort(dst, stable=True)
        src = src[_o]
        dst = dst[_o]
        edge_type_8 = jax.random.randint(jax.random.fold_in(_gk, 12), (400000,), 0, 8, jnp.int32)
        edge_weight = jax.random.uniform(jax.random.fold_in(_gk, 13), (400000,), jnp.float32, 0.0, 1)
        return (x, src, dst, edge_type_8, edge_weight)
    x, src, dst, edge_type_8, edge_weight = _rec_inputs()

    def _L0_gnn_setup():
        import jax, jax.numpy as jnp
        import numpy as np
        N = 12500
        E = 100000
        D = 128
        key = jax.random.key(seed)
        ks = jax.random.split(key, 12)
        s = lambda fan_in: 1.0 / np.sqrt(fan_in)
        return {'h': jax.random.normal(ks[0], (N, D), dtype=jnp.float32), 'w': jax.random.uniform(ks[1], (E,), dtype=jnp.float32), 'src': jax.random.randint(ks[2], (E,), 0, N, dtype=jnp.int32), 'dst': jax.random.randint(ks[3], (E,), 0, N, dtype=jnp.int32), 'W1': jax.random.uniform(ks[4], (2 * D + 1, D), jnp.float32, -s(2 * D + 1), s(2 * D + 1)), 'b1': jnp.zeros((D,), jnp.float32), 'W2': jax.random.uniform(ks[5], (D, D), jnp.float32, -s(D), s(D)), 'b2': jnp.zeros((D,), jnp.float32), 'U1': jax.random.uniform(ks[6], (2 * D, D), jnp.float32, -s(2 * D), s(2 * D)), 'c1': jnp.zeros((D,), jnp.float32), 'U2': jax.random.uniform(ks[7], (D, D), jnp.float32, -s(D), s(D)), 'c2': jnp.zeros((D,), jnp.float32)}
    _L0_gnn_all = _L0_gnn_setup()
    _L0_gnn_in = {k: v for k, v in _L0_gnn_all.items() if k in ('W1', 'b1', 'W2', 'b2', 'U1', 'c1', 'U2', 'c2')}
    del _L0_gnn_all

    def _L1_gnn_setup():
        import jax, jax.numpy as jnp
        import numpy as np
        N_NODES = 12500
        N_EDGES = 75000
        IN_FEAT = 128
        OUT_FEAT = 128
        NUM_RELS = 8
        NUM_BASES = 4
        key = jax.random.key(seed)
        ks = jax.random.split(key, 8)
        h = jax.random.normal(ks[0], (N_NODES, IN_FEAT), dtype=jnp.float32)
        weight = jax.random.normal(ks[1], (NUM_BASES, IN_FEAT, OUT_FEAT), dtype=jnp.float32) * (1.0 / np.sqrt(IN_FEAT))
        w_comp = jax.random.normal(ks[2], (NUM_RELS, NUM_BASES), dtype=jnp.float32) * (1.0 / np.sqrt(NUM_BASES))
        root_weight = jax.random.normal(ks[3], (IN_FEAT, OUT_FEAT), dtype=jnp.float32) * (1.0 / np.sqrt(IN_FEAT))
        bias = jnp.zeros((OUT_FEAT,), dtype=jnp.float32)
        src = jax.random.randint(ks[4], (N_EDGES,), 0, N_NODES, dtype=jnp.int32)
        dst = jax.random.randint(ks[5], (N_EDGES,), 0, N_NODES, dtype=jnp.int32)
        rel_type = jax.random.randint(ks[6], (N_EDGES,), 0, NUM_RELS, dtype=jnp.int32)
        return {'h': h, 'weight': weight, 'w_comp': w_comp, 'root_weight': root_weight, 'bias': bias, 'src': src, 'dst': dst, 'rel_type': rel_type}
    _L1_gnn_all = _L1_gnn_setup()
    _L1_gnn_in = {k: v for k, v in _L1_gnn_all.items() if k in ('weight', 'w_comp', 'root_weight', 'bias')}
    del _L1_gnn_all
    return {'x': x, 'src': src, 'dst': dst, 'edge_type_8': edge_type_8, 'edge_weight': edge_weight, 'L0_gnn_W1': _L0_gnn_in['W1'], 'L0_gnn_b1': _L0_gnn_in['b1'], 'L0_gnn_W2': _L0_gnn_in['W2'], 'L0_gnn_b2': _L0_gnn_in['b2'], 'L0_gnn_U1': _L0_gnn_in['U1'], 'L0_gnn_c1': _L0_gnn_in['c1'], 'L0_gnn_U2': _L0_gnn_in['U2'], 'L0_gnn_c2': _L0_gnn_in['c2'], 'L1_gnn_weight': _L1_gnn_in['weight'], 'L1_gnn_w_comp': _L1_gnn_in['w_comp'], 'L1_gnn_root_weight': _L1_gnn_in['root_weight'], 'L1_gnn_bias': _L1_gnn_in['bias']}

def reference(x, src, dst, edge_type_8, edge_weight, L0_gnn_W1, L0_gnn_b1, L0_gnn_W2, L0_gnn_b2, L0_gnn_U1, L0_gnn_c1, L0_gnn_U2, L0_gnn_c2, L1_gnn_weight, L1_gnn_w_comp, L1_gnn_root_weight, L1_gnn_bias):
    import jax
    import jax.numpy as jnp

    def _L0_gnn_ref(h, w, src, dst, W1, b1, W2, b2, U1, c1, U2, c2):
        import jax, jax.numpy as jnp
        import numpy as np
        N = 12500
        E = 100000
        D = 128
        n = h.shape[0]
        msg_in = jnp.concatenate([h[src], h[dst], w[:, None]], axis=1)
        msg = jax.nn.relu(msg_in @ W1 + b1) @ W2 + b2
        agg = jax.ops.segment_max(msg, dst, num_segments=n)
        deg = jax.ops.segment_sum(jnp.ones((dst.shape[0],), jnp.int32), dst, num_segments=n)
        agg = jnp.where((deg > 0)[:, None], agg, jnp.zeros((), h.dtype))
        upd_in = jnp.concatenate([h, agg], axis=1)
        return jax.nn.relu(upd_in @ U1 + c1) @ U2 + c2

    def _L1_gnn_ref(h, weight, w_comp, root_weight, bias, src, dst, rel_type):
        import jax, jax.numpy as jnp
        import numpy as np
        N_NODES = 12500
        N_EDGES = 75000
        IN_FEAT = 128
        OUT_FEAT = 128
        NUM_RELS = 8
        NUM_BASES = 4
        B, I, O = weight.shape
        R = w_comp.shape[0]
        W = (w_comp @ weight.reshape(B, I * O)).reshape(R, I, O)
        proj = jnp.einsum('ni,rio->nro', h, W)
        msg = proj[src, rel_type]
        agg = jax.ops.segment_sum(msg, dst, num_segments=h.shape[0])
        out = h @ root_weight + agg + bias
        return jax.nn.relu(out)
    h = jnp.maximum(_layernorm(x, axis=-1), 0.0)
    x = x + _L0_gnn_ref(h, edge_weight, src, dst, L0_gnn_W1, L0_gnn_b1, L0_gnn_W2, L0_gnn_b2, L0_gnn_U1, L0_gnn_c1, L0_gnn_U2, L0_gnn_c2)
    h = jnp.maximum(_layernorm(x, axis=-1), 0.0)
    x = x + _L1_gnn_ref(h, L1_gnn_weight, L1_gnn_w_comp, L1_gnn_root_weight, L1_gnn_bias, src, dst, edge_type_8)
    return x

_drawn_inputs = setup_inputs


def setup_inputs(seed=0):
    import zlib

    import numpy as np

    out = dict(_drawn_inputs(seed))
    spreads = {'L0_gnn_b1': (0.0, 0.8),
     'L0_gnn_b2': (0.0, 0.413),
     'L0_gnn_c1': (0.0, 0.1),
     'L0_gnn_c2': (0.0, 0.1),
     'L1_gnn_bias': (0.0, 0.539)}
    factors = {'edge_weight': 130.328, 'L0_gnn_W1': 3.807}
    for name, (base, spread) in spreads.items():
        noise = np.random.default_rng([zlib.crc32(name.encode()), seed]).standard_normal(out[name].shape)
        drawn = base * np.exp(spread * noise) if base else spread * noise
        out[name] = jnp.asarray(drawn.astype(out[name].dtype))
    for name, factor in factors.items():
        out[name] = (out[name] * factor).astype(out[name].dtype)
    return out
```

```python
import concourse.bass as bass
from concourse import mybir
from contextlib import ExitStack

P = 128
GT = 4
GE = GT * P
GPI = 4
TPI = GT * GPI



def after(eng, sem, n):
    if not (isinstance(n, int) and n <= 0):
        eng.wait_ge(sem, n)


def there(k):
    return not (isinstance(k, int) and k < 0)


def gnn(nc, x, dst, src_cols, dst_cols, type_cols, w, W1, b1, W2, b2, U1, c1, U2, c2,
        basis, comp, root, bias, out):
    fp32, bf16, i32 = mybir.dt.float32, mybir.dt.bfloat16, mybir.dt.int32
    ALU, ACT, AX = mybir.AluOpType, mybir.ActivationFunctionType, mybir.AxisListType
    RMAX = bass.bass_isa.ReduceOp.max

    NP, D = x.shape
    NT = NP // P
    ET = src_cols.shape[1]
    EP = ET * P
    ITERS = ET // TPI
    NGRP = ITERS * GPI
    NB, _, _ = basis.shape
    NR = comp.shape[0]
    CH = 7
    NCH = NT // CH
    CW = CH * P
    MP = 112
    MT = ET // MP
    HALF = 2 * GE
    SPREAD = NP + P
    EPS = 1e-5
    LOW = 3.0e38
    NOROW = 1 << 20
    assert NT % (2 * CH) == 0 and ET % MP == 0 and D == P and ITERS >= 3

    p_tab = nc.dram_tensor("p_tab", (NP, D), fp32).ap()
    q_tab = nc.dram_tensor("q_tab", (SPREAD + EP, D), fp32).ap()
    proj_tab = nc.dram_tensor("proj_tab", (NP * NR, D), fp32).ap()
    run_tab = nc.dram_tensor("run_tab", (EP, D), fp32).ap()
    marks = nc.dram_tensor("marks", (3, EP), bf16).ap()
    win_tab = nc.dram_tensor("win_tab", (1, ET), i32).ap()
    last_tab = nc.dram_tensor("last_tab", (P, P), i32).ap()
    has_tab = nc.dram_tensor("has_tab", (P, P), fp32).ap()

    p_rows = p_tab.rearrange("(p t) d -> p t d", p=P)
    q_rows = q_tab[0:NP, :].rearrange("(p t) d -> p t d", p=P)
    x_rows = x.rearrange("(p t) d -> p t d", p=P)
    out_rows = out.rearrange("(p t) d -> p t d", p=P)
    proj_rows = proj_tab.rearrange("(p t r) d -> p t (r d)", p=P, r=NR)
    run_rows = run_tab.rearrange("(g p j) d -> p g (j d)", p=P, j=GT)

    ctx = ExitStack()

    def sem(name):
        return ctx.enter_context(nc.semaphore(name))

    def tensors(stack):
        def sb(name, shape, dt):
            return stack.enter_context(nc.sbuf_tensor(name, shape, dt))

        def ps(name, shape):
            return stack.enter_context(nc.psum_tensor(name, shape, fp32))
        return sb, ps

    def row(v):
        return v.rearrange("(a n) -> a n", a=1)

    def col(v):
        return v.rearrange("(n a) -> n a", a=1)

    def pairs(eng, step):
        for u in range(2):
            step(0, u)
        with eng.Fori(1, NCH // 2 - 1) as i:
            for u in range(2):
                step(i, u)
        for u in range(2):
            step(NCH // 2 - 1, u)

    def sweep(eng, step):
        for s in range(GPI):
            step(0, s)
        with eng.Fori(1, ITERS - 1) as i:
            for s in range(GPI):
                step(i, s)
        for s in range(GPI):
            step(ITERS - 1, s)

    with ctx:
        keep, _ = tensors(ctx)
        xa = keep("xa", [P, NT, D], fp32)
        hT = keep("hT", [P, NT * P], fp32)
        ident = keep("ident", [P, P], fp32)
        idx1 = keep("idx1", [P, ET], i32)
        cnt = keep("cnt", [P, P], fp32)
        last = keep("last", [P, NT], i32)
        has = keep("has", [P, NT], fp32)
        edge_keep = ctx.enter_context(ExitStack())
        ekeep, _ = tensors(edge_keep)
        idx0 = ekeep("idx0", [P, ET], i32)
        hiB = ekeep("hiB", [P, ET], bf16)
        loB = ekeep("loB", [P, ET], bf16)

        with ExitStack() as ph:
            sb, ps = tensors(ph)
            w1ab = sb("w1ab", [P, 2, D], fp32)
            xsum = sb("xsum", [P, 2, CH], fp32)
            xvar = sb("xvar", [P, 2, CH], fp32)
            std = sb("std", [P, 2, CH], fp32)
            rstd = sb("rstd", [P, 2, CH], fp32)
            epsc = sb("epsc", [P, 1], fp32)
            hn = sb("hn", [P, 2, CH, D], fp32)
            hs = sb("hs", [P, CW], fp32)
            pq = sb("pq", [P, CH, 2, D], fp32)
            dI = sb("dI", [P, MT * P], i32)
            rel = sb("rel", [MP, MT, P], fp32)
            cont = sb("cont", [MP, MT, P], bf16)
            lowm = sb("lowm", [MP, MT, P], bf16)
            relb = sb("relb", [MP, MT, P], bf16)
            ext = sb("ext", [P, 2], fp32)
            exta = sb("exta", [P, 2], fp32)
            wide = sb("wide", [P, 4], fp32)
            wideI = sb("wideI", [P, 1], i32)
            place = sb("place", [MP, P], fp32)
            place_fix = sb("place_fix", [MP, P], fp32)
            tile0 = sb("tile0", [MP, MT], fp32)
            winI = sb("winI", [MP, MT], i32)
            spI = sb("spI", [P, 1], i32)
            spR = sb("spR", [P, D], fp32)
            psH = ps("psH", [P, 1024])
            psQ = ps("psQ", [P, 2048])
            psS = ps("psS", [P, 1024])

            x_loaded = sem("x_loaded")
            w1_loaded = sem("w1_loaded")
            idx_loaded = sem("idx_loaded")
            types_loaded = sem("types_loaded")
            dst_loaded = sem("dst_loaded")
            prev_loaded = sem("prev_loaded")
            cols_loaded = sem("cols_loaded")
            cols_again = sem("cols_again")
            pad_zeroed = sem("pad_zeroed")
            ident_zeroed = sem("ident_zeroed")
            ident_ready = sem("ident_ready")
            iota_ready = sem("iota_ready")
            eps_ready = sem("eps_ready")
            xsum_done = sem("xsum_done")
            centered = sem("centered")
            squared = sem("squared")
            xvar_done = sem("xvar_done")
            std_done = sem("std_done")
            rstd_done = sem("rstd_done")
            normed = sem("normed")
            h_transposed = sem("h_transposed")
            h_relu = sem("h_relu")
            h_kept = sem("h_kept")
            pq_done = sem("pq_done")
            pq_copied_a = sem("pq_copied_a")
            pq_copied_b = sem("pq_copied_b")
            p_stored = sem("p_stored")
            q_stored = sem("q_stored")
            idx1_done = sem("idx1_done")
            mark_step = sem("mark_step")
            extent_ready = sem("extent_ready")
            extent_joined = sem("extent_joined")
            hi_done = sem("hi_done")
            lo_done = sem("lo_done")
            marks_stored = sem("marks_stored")
            win_stored = sem("win_stored")
            spread_idx = sem("spread_idx")
            spread_got = sem("spread_got")
            spread_stored = sem("spread_stored")

            dI3 = dI[0:MP, :].rearrange("p (t e) -> p t e", e=P)
            prev = rel[:, :, :].bitcast(i32)
            dcol = dI[:, 0:ET]
            with nc.Block() as block:
                @block.sync
                def _(sp):
                    for a in range(2):
                        sp.dma_start(w1ab[:, a, :], W1[a * D:(a + 1) * D, :]).then_inc(w1_loaded, 16)
                        sp.wait_ge(w1_loaded, 16 * (a + 1))
                    sp.dma_start(xa[:, :, :], x_rows).then_inc(x_loaded, 16)
                    sp.dma_start(idx0[:, :], src_cols).then_inc(idx_loaded, 16)
                    sp.dma_start(idx1[:, :], type_cols).then_inc(types_loaded, 16)
                    sp.dma_start(dI3, dst[1:EP + 1].rearrange("(p t e) -> p t e", p=MP, e=P)).then_inc(dst_loaded, 16)
                    sp.dma_start(prev, dst[0:EP].rearrange("(p t e) -> p t e", p=MP, e=P)).then_inc(prev_loaded, 16)

                    def store(c):
                        sp.wait_ge(pq_copied_a, c + 1)
                        sp.wait_ge(pq_copied_b, c + 1)
                        sp.dma_start(p_rows[:, bass.ds(c * CH, CH), :], pq[:, :, 0, :]).then_inc(p_stored, 16)
                        sp.dma_start(q_rows[:, bass.ds(c * CH, CH), :], pq[:, :, 1, :]).then_inc(q_stored, 16)
                    with sp.Fori(0, NCH) as c:
                        store(c)
                    sp.wait_ge(mark_step, 10)
                    for n, t in enumerate((relb, lowm, cont)):
                        sp.dma_start(marks[n, :].rearrange("(p t e) -> p t e", p=MP, e=P), t[:, :, :]).then_inc(marks_stored, 16)
                    sp.dma_start(win_tab.rearrange("a (p t) -> (a p) t", p=MP), winI[:, :]).then_inc(win_stored, 16)
                    sp.dma_start(dcol, dst_cols).then_inc(cols_loaded, 16)
                    sp.wait_ge(hi_done, 2)
                    sp.dma_start(dcol, dst_cols).then_inc(cols_again, 16)
                    sp.wait_ge(pad_zeroed, 1)
                    sp.dma_start(q_tab[NP:SPREAD, :], spR[:, :]).then_inc(q_stored, 16)
                    sp.wait_ge(p_stored, 16 * NCH)
                    sp.wait_ge(q_stored, 16 * NCH + 16)
                    sp.wait_ge(marks_stored, 48)
                    sp.wait_ge(win_stored, 16)

                @block.gpsimd
                def _(pool):
                    pool.memset(ident[:, :], 0.0).then_inc(ident_zeroed, 1)
                    pool.wait_ge(ident_zeroed, 1)
                    pool.affine_select(out=ident[:, :], in_=ident[:, :], compare_op=ALU.not_equal, fill=1.0,
                                       base=0, pattern=[[-1, P]], channel_multiplier=1).then_inc(ident_ready, 1)
                    pool.iota(place[:, :], pattern=[[1, P]], base=0, channel_multiplier=0,
                              allow_small_or_imprecise_dtypes=True)
                    pool.iota(tile0[:, :], pattern=[[P, MT]], base=SPREAD, channel_multiplier=P * MT,
                              allow_small_or_imprecise_dtypes=True).then_inc(iota_ready, 1)
                    pool.memset(spR[:, :], 0.0).then_inc(pad_zeroed, 1)
                    pool.wait_ge(extent_ready, 3)
                    pool.partition_all_reduce(exta[:, :], ext[:, :], P, RMAX).then_inc(extent_joined, 1)

                @block.scalar
                def _(act):
                    act.wait_ge(eps_ready, 1)

                    def square(k, u):
                        act.wait_ge(centered, k + 1)
                        after(act, xvar_done, k)
                        nc.scalar.activation(psS[:, 0:CW], hn[:, u, :, :].rearrange("p t d -> p (t d)"), ACT.Square).then_inc(squared, 1)

                    def deviation(k, u):
                        act.wait_ge(xvar_done, k + 1)
                        nc.scalar.activation(std[:, u, :], xvar[:, u, :], ACT.Sqrt, bias=epsc[:, 0:1], scale=1.0 / D).then_inc(std_done, 1)

                    def relu(k):
                        act.wait_ge(h_transposed, k + 1)
                        after(act, pq_done, k)
                        nc.scalar.activation(hs[:, :], psH[:, 0:CW], ACT.Relu).then_inc(h_relu, 1)
                        nc.scalar.activation(hT[:, bass.ds(k * CW, CW)], psH[:, 0:CW], ACT.Relu).then_inc(h_kept, 1)

                    def copy_pq(k):
                        act.wait_ge(pq_done, k + 1)
                        after(act, p_stored, k * 16)
                        after(act, q_stored, k * 16)
                        nc.scalar.activation(pq[:, 0:4, :, :].rearrange("p t a d -> p (t a d)"), psQ[:, 0:1024],
                                             ACT.Copy).then_inc(pq_copied_a, 1)
                    square(0, 0)

                    def step(i, u):
                        k = 2 * i + u
                        if not (isinstance(k, int) and k + 1 >= NCH):
                            square(k + 1, 1 - u)
                        deviation(k, u)
                        if there(k - 1):
                            copy_pq(k - 1)
                        relu(k)
                    pairs(act, step)
                    copy_pq(NCH - 1)

                @block.tensor
                def _(pe):
                    pe.wait_ge(ident_ready, 1)
                    pe.wait_ge(w1_loaded, 32)

                    def step(i, u):
                        k = 2 * i + u
                        pe.wait_ge(normed, k + 1)
                        after(pe, h_kept, k)
                        for t in range(CH):
                            ins = nc.tensor.transpose(psH[:, t * P:(t + 1) * P], hn[:, u, t, :], ident[:, :])
                        ins.then_inc(h_transposed, 1)
                        pe.wait_ge(h_relu, k + 1)
                        after(pe, pq_copied_a, k)
                        after(pe, pq_copied_b, k)
                        for t in range(CH):
                            ins = nc.tensor.matmul(psQ[:, t * 2 * D:(t + 1) * 2 * D], hs[:, t * P:(t + 1) * P],
                                                   w1ab[:, :, :].rearrange("p a d -> p (a d)"), start=True, stop=True)
                        ins.then_inc(pq_done, 1)
                    pairs(pe, step)

                @block.vector
                def _(dve):
                    nc.vector.memset(epsc[:, :], EPS).then_inc(eps_ready, 1)
                    nc.vector.memset(ext[:, :], 0.0).then_inc(extent_ready, 1)
                    dve.wait_ge(x_loaded, 16)

                    def center(k, u):
                        xc = xa[:, bass.ds(k * CH, CH), :]
                        nc.vector.tensor_reduce(xsum[:, u, :], xc, AX.X, ALU.add).then_inc(xsum_done, 1)
                        dve.wait_ge(xsum_done, k + 1)
                        if there(k - 2):
                            dve.wait_ge(h_transposed, k - 1)
                        nc.vector.scalar_tensor_tensor(out=hn[:, u, :, :], in0=xsum[:, u, :].unsqueeze(2).to_broadcast([P, CH, D]),
                                                       scalar=-1.0 / D, in1=xc, op0=ALU.mult, op1=ALU.add).then_inc(centered, 1)

                    def scale(k, u):
                        dve.wait_ge(std_done, k + 1)
                        nc.vector.reciprocal(rstd[:, u, :], std[:, u, :]).then_inc(rstd_done, 1)
                        dve.wait_ge(rstd_done, k + 1)
                        nc.vector.tensor_tensor(hn[:, u, :, :], hn[:, u, :, :], rstd[:, u, :].unsqueeze(2).to_broadcast([P, CH, D]),
                                                ALU.mult).then_inc(normed, 1)

                    def variance(k, u):
                        dve.wait_ge(squared, k + 1)
                        nc.vector.tensor_reduce(xvar[:, u, :], psS[:, 0:CW].rearrange("p (t d) -> p t d", t=CH), AX.X,
                                                ALU.add).then_inc(xvar_done, 1)

                    def copy_pq(k):
                        dve.wait_ge(pq_done, k + 1)
                        after(dve, p_stored, k * 16)
                        after(dve, q_stored, k * 16)
                        nc.vector.tensor_copy(pq[:, 4:CH, :, :].rearrange("p t a d -> p (t a d)"),
                                              psQ[:, 1024:CH * 2 * D]).then_inc(pq_copied_b, 1)
                    center(0, 0)

                    def step(i, u):
                        k = 2 * i + u
                        variance(k, u)
                        if not (isinstance(k, int) and k + 1 >= NCH):
                            dve.nop(nofuse=True)
                            center(k + 1, 1 - u)
                        scale(k, u)
                        if there(k - 1):
                            copy_pq(k - 1)
                    pairs(dve, step)
                    copy_pq(NCH - 1)

                    dve.wait_ge(idx_loaded, 16)
                    dve.wait_ge(types_loaded, 16)
                    nc.vector.scalar_tensor_tensor(out=idx1[:, :], in0=idx0[:, :], scalar=float(NR), in1=idx1[:, :],
                                                   op0=ALU.mult, op1=ALU.add).then_inc(idx1_done, 1)

                    done = [0]

                    def mark(ins):
                        done[0] += 1
                        ins.then_inc(mark_step, 1)
                        dve.wait_ge(mark_step, done[0])
                    dve.wait_ge(dst_loaded, 16)
                    dve.wait_ge(prev_loaded, 16)
                    mark(nc.vector.tensor_tensor(cont[:, :, :], dI3, prev, ALU.is_equal))
                    mark(nc.vector.tensor_scalar(lowm[:, :, :], cont[:, :, :], -1.0, LOW, ALU.add, ALU.mult))
                    mark(nc.vector.tensor_tensor(rel[:, :, :], dI3, dI3[:, :, 0:1].to_broadcast([MP, MT, P]), ALU.subtract))
                    dve.wait_ge(extent_ready, 1)
                    nc.vector.tensor_reduce(ext[0:MP, 0:1], rel[:, :, :], AX.XY, ALU.max).then_inc(extent_ready, 1)
                    nc.vector.tensor_reduce(ext[0:MP, 1:2], rel[:, :, :], AX.XY, ALU.min, negate=True).then_inc(extent_ready, 1)
                    dve.wait_ge(extent_joined, 1)
                    mark(nc.vector.tensor_scalar(wide[:, 0:1], exta[:, 0:1], float(P - 1), None, ALU.is_gt))
                    mark(nc.vector.tensor_scalar(wide[:, 1:2], exta[:, 1:2], 0.0, None, ALU.is_gt))
                    mark(nc.vector.tensor_tensor(wide[:, 2:3], wide[:, 0:1], wide[:, 1:2], ALU.max))
                    nc.vector.tensor_copy(wideI[:, :], wide[:, 2:3])
                    mark(nc.vector.tensor_scalar(wide[:, 3:4], wide[:, 2:3], -1.0, 1.0, ALU.mult, ALU.add))
                    dve.wait_ge(iota_ready, 1)
                    nc.vector.tensor_scalar(place_fix[:, :], place[:, :], wide[0:MP, 2:3], None, ALU.mult)
                    mark(nc.vector.tensor_scalar(tile0[:, :], tile0[:, :], wide[0:MP, 2:3], None, ALU.mult))
                    nc.vector.scalar_tensor_tensor(out=winI[:, :], in0=dI3[:, :, 0], scalar=wide[0:MP, 3:4], in1=tile0[:, :],
                                                   op0=ALU.mult, op1=ALU.add)
                    mark(nc.vector.scalar_tensor_tensor(out=relb[:, :, :], in0=rel[:, :, :], scalar=wide[0:MP, 3:4],
                                                        in1=place_fix[:, :].unsqueeze(1).to_broadcast([MP, MT, P]),
                                                        op0=ALU.mult, op1=ALU.add))
                    nc.vector.memset(cnt[:, :], 0.0).then_inc(mark_step, 1)
                    dve.wait_ge(cols_loaded, 16)
                    nc.vector.tensor_scalar(dcol, dcol, 7, None, ALU.logical_shift_right).then_inc(hi_done, 1)
                    dve.wait_ge(hi_done, 1)
                    nc.vector.tensor_copy(hiB[:, :], dcol).then_inc(hi_done, 1)
                    dve.wait_ge(cols_again, 16)
                    nc.vector.tensor_scalar(dcol, dcol, P - 1, None, ALU.bitwise_and).then_inc(lo_done, 1)
                    dve.wait_ge(lo_done, 1)
                    nc.vector.tensor_copy(loB[:, :], dcol).then_inc(lo_done, 1)

            with nc.Block() as block:
                @block.gpsimd
                def _(pool):
                    flag = pool.value_load(wideI[0:1, 0:1], min_val=0, max_val=1)
                    with pool.If(flag):
                        with pool.Fori(0, ET) as t:
                            pool.dma_start(spI[:, :], col(dst[bass.ds(t * P + 1, P)])).then_inc(spread_idx, 16)
                            pool.wait_ge(spread_idx, (t + 1) * 16)
                            pool.nop(nofuse=True)
                            pool.indirect_dma_start(spR[:, :], None, q_tab[0:NP, :],
                                                    bass.IndirectOffsetOnAxis(ap=spI[:, 0:1], axis=0)).then_inc(spread_got, 16)
                            pool.wait_ge(spread_got, (t + 1) * 16)
                            pool.dma_start(q_tab[bass.ds(SPREAD + t * P, P), :], spR[:, :]).then_inc(spread_stored, 16)
                            pool.wait_ge(spread_stored, (t + 1) * 16)
                            pool.nop(nofuse=True)

        with ExitStack() as ph:
            sb, ps = tensors(ph)
            G = sb("G", [P, GPI, GT, D], fp32)
            Qw = sb("Qw", [P, GPI, GT, D], fp32)
            oh = sb("oh", [P, 2, GE], fp32)
            Z = sb("Z", [P, 2, GE], fp32)
            R = sb("R", [P, 2, GE], fp32)
            O = sb("O", [P, 2, GE], fp32)
            mk = sb("mk", [P, 2, 2, HALF], bf16)
            wz = sb("wz", [P, 2, HALF], fp32)
            hoh = sb("hoh", [P, 2, 2, GE], bf16)
            idxs = sb("idxs", [P, GPI, GT], i32)
            win = sb("win", [1, ET], i32)
            pidx = sb("pidx", [P, 1], fp32)
            lane = sb("lane", [P, P], bf16)
            w1c = sb("w1c", [P, D], fp32)
            w2 = sb("w2", [P, D], fp32)
            b1c = sb("b1c", [P, 1], fp32)
            psZ = ps("psZ", [P, 2, GE])
            psM = ps("psM", [P, 2, GE])
            psB = ps("psB", [P, 2, GE])
            psC = ps("psC", [P, GE])

            consts = sem("consts")
            zeroed = sem("zeroed")
            iota2 = sem("iota2")
            w2_loaded = sem("w2_loaded")
            w1c_loaded = sem("w1c_loaded")
            b1_loaded = sem("b1_loaded")
            win_loaded = sem("win_loaded")
            idx_ready = sem("idx_ready")
            gathered = [sem(f"gathered{n}") for n in range(GPI)]
            qwin_loaded = [sem(f"qwin_loaded{n}") for n in range(GPI)]
            marks_loaded = [sem(f"marks_loaded{n}") for n in range(2)]
            wgt_loaded = [sem(f"wgt_loaded{n}") for n in range(2)]
            onehot_ready = sem("onehot_ready")
            z_done = sem("z_done")
            relu_done = sem("relu_done")
            msg_done = sem("msg_done")
            scanned = sem("scanned")
            back_done = sem("back_done")
            back_copied = sem("back_copied")
            stored = [sem(f"stored{n}") for n in range(2)]
            counted = sem("counted")

            with nc.Block() as block:
                @block.sync
                def _(sp):
                    sp.dma_start(win[:, :], win_tab).then_inc(win_loaded, 16)
                    sp.dma_start(w2[:, :], W2).then_inc(w2_loaded, 16)
                    sp.dma_start(b1c[:, :], col(b1)).then_inc(b1_loaded, 16)
                    sp.wait_ge(zeroed, 2)
                    sp.dma_start(w1c[0:1, :], W1[2 * D:2 * D + 1, :]).then_inc(w1c_loaded, 16)
                    sp.wait_ge(win_loaded, 16)

                    def step(i, s):
                        k = GPI * i + s
                        if s % 2 == 0:
                            h = s // 2
                            e = (GPI * i + s) * GE
                            if there(k - GPI):
                                sp.wait_ge(scanned, k - 1)
                            sp.dma_start(mk[:, h, :, :],
                                         marks[0:2, bass.ds(e, HALF)].partition_broadcast(P)).then_inc(marks_loaded[h], 16)
                            sp.dma_start(wz[0:1, h, :], row(w)[:, bass.ds(e, HALF)]).then_inc(wgt_loaded[h], 16)
                        if there(k - GPI):
                            sp.wait_ge(z_done, k - GPI + 1)
                        for j in range(GT):
                            r0 = sp.value_load(win[0:1, bass.ds(k * GT + j, 1)], min_val=0, max_val=SPREAD + EP - P)
                            sp.dma_start(Qw[:, s, j, :], q_tab[bass.ds(r0, P), :]).then_inc(qwin_loaded[s], 16)
                    sweep(sp, step)

                @block.gpsimd
                def _(pool):
                    pool.iota(pidx[:, :], pattern=[[0, 1]], base=0, channel_multiplier=1,
                              allow_small_or_imprecise_dtypes=True)
                    pool.iota(lane[:, :], pattern=[[1, P]], base=0, channel_multiplier=0,
                              allow_small_or_imprecise_dtypes=True).then_inc(iota2, 1)

                    def step(i, s):
                        k = GPI * i + s
                        pool.wait_ge(idx_ready, k + 1)
                        pool.nop(nofuse=True)
                        if there(k - GPI):
                            pool.wait_ge(z_done, k - GPI + 1)
                            pool.nop(nofuse=True)
                        for j in range(GT):
                            pool.indirect_dma_start(G[:, s, j, :], None, p_tab,
                                                    bass.IndirectOffsetOnAxis(ap=idxs[:, s, j:j + 1], axis=0)
                                                    ).then_inc(gathered[s], 16)
                    sweep(pool, step)

                @block.tensor
                def _(pe):
                    pe.wait_ge(w2_loaded, 16)
                    pe.wait_ge(w1c_loaded, 16)
                    pe.wait_ge(zeroed, 2)

                    def z(i, s):
                        k, b = GPI * i + s, s % 2
                        pe.wait_ge(onehot_ready, k + 1)
                        pe.wait_ge(wgt_loaded[s // 2], 16 * (i + 1))
                        if there(k - 2):
                            pe.wait_ge(relu_done, k - 1)
                        nc.tensor.matmul(psZ[:, b, :], w1c[:, :], wz[:, s // 2, b * GE:(b + 1) * GE], start=True, stop=False)
                        for j in range(GT):
                            nc.tensor.matmul(psC[:, 0:P], hoh[:, b, 0, j * P:(j + 1) * P], hoh[:, b, 1, j * P:(j + 1) * P],
                                             start=isinstance(k, int) and k + j == 0,
                                             stop=isinstance(k, int) and k == NGRP - 1 and j == GT - 1)
                        pe.wait_ge(qwin_loaded[s], 16 * GT * (i + 1))
                        for j in range(GT):
                            nc.tensor.matmul(psZ[:, b, j * P:(j + 1) * P], Qw[:, s, j, :], oh[:, b, j * P:(j + 1) * P],
                                             start=False, stop=False)
                        pe.wait_ge(gathered[s], 16 * GT * (i + 1))
                        for j in range(GT):
                            ins = nc.tensor.matmul(psZ[:, b, j * P:(j + 1) * P], G[:, s, j, :], ident[:, :],
                                                   start=False, stop=j == GT - 1)
                        ins.then_inc(z_done, 1)

                    def msg(k, b):
                        pe.wait_ge(relu_done, k + 1)
                        if there(k - 2):
                            pe.wait_ge(scanned, k)
                        nc.tensor.matmul(psM[:, b, :], w2[:, :], Z[:, b, :], start=True, stop=True).then_inc(msg_done, 1)

                    def back(k, b):
                        pe.wait_ge(scanned, k + 2)
                        if there(k - 2):
                            pe.wait_ge(back_copied, k - 1)
                        for j in range(GT):
                            ins = nc.tensor.transpose(psB[:, b, j * P:(j + 1) * P], R[:, b, j * P:(j + 1) * P], ident[:, :])
                        ins.then_inc(back_done, 1)

                    def step(i, s):
                        k = GPI * i + s
                        z(i, s)
                        if there(k - 1):
                            msg(k - 1, (s + 1) % 2)
                        if there(k - 2):
                            back(k - 2, s % 2)
                    sweep(pe, step)
                    msg(NGRP - 1, 1)
                    back(NGRP - 2, 0)
                    back(NGRP - 1, 1)

                @block.scalar
                def _(act):
                    act.wait_ge(b1_loaded, 16)

                    def relu(k, b):
                        act.wait_ge(z_done, k + 1)
                        if there(k - 2):
                            act.wait_ge(msg_done, k - 1)
                        nc.scalar.activation(Z[:, b, :], psZ[:, b, :], ACT.Relu, bias=b1c[:, 0:1]).then_inc(relu_done, 1)

                    def put(k, b, n):
                        act.wait_ge(back_done, k + 1)
                        after(act, stored[b], 16 * n)
                        nc.scalar.activation(O[:, b, :], psB[:, b, :], ACT.Copy).then_inc(back_copied, 1)
                        act.wait_ge(back_copied, k + 1)
                        act.dma_start(run_rows[:, bass.ds(k, 1), :].rearrange("p g d -> p (g d)"), O[:, b, :]).then_inc(stored[b], 16)

                    def step(i, s):
                        k = GPI * i + s
                        relu(k, s % 2)
                        if there(k - 2):
                            put(k - 2, s % 2, 2 * i + s // 2 - 1)
                    sweep(act, step)
                    put(NGRP - 2, 0, NGRP // 2 - 1)
                    put(NGRP - 1, 1, NGRP // 2 - 1)
                    for b in range(2):
                        act.wait_ge(stored[b], 16 * (NGRP // 2))

                @block.vector
                def _(dve):
                    nc.vector.memset(wz[:, :, :], 0.0).then_inc(zeroed, 1)
                    nc.vector.memset(w1c[:, :], 0.0).then_inc(zeroed, 1)
                    nc.vector.memset(R[:, 1, :], 0.0).then_inc(scanned, 1)
                    dve.wait_ge(iota2, 1)

                    def indices(i, s):
                        k = GPI * i + s
                        if there(k - GPI):
                            dve.wait_ge(gathered[s], 16 * GT * i)
                        nc.vector.tensor_copy(idxs[:, s, :], idx0[:, bass.ds(k * GT, GT)]).then_inc(idx_ready, 1)

                    def onehot(i, s):
                        k, b = GPI * i + s, s % 2
                        if there(k - 2):
                            dve.wait_ge(z_done, k - 1)
                        for a, half in enumerate((hiB, loB)):
                            nc.vector.tensor_tensor(hoh[:, b, a, :].rearrange("p (j e) -> p j e", j=GT),
                                                    lane[:, :].unsqueeze(1).to_broadcast([P, GT, P]),
                                                    half[:, bass.ds(k * GT, GT)].unsqueeze(2).to_broadcast([P, GT, P]),
                                                    ALU.is_equal)
                        dve.wait_ge(marks_loaded[s // 2], 16 * (i + 1))
                        nc.vector.tensor_scalar(oh[:, b, :], mk[:, s // 2, 0, b * GE:(b + 1) * GE], pidx[:, 0:1], None,
                                                ALU.is_equal).then_inc(onehot_ready, 1)

                    def scan(k, s):
                        b = s % 2
                        dve.wait_ge(msg_done, k + 1)
                        dve.wait_ge(scanned, k + 1)
                        if there(k - 2):
                            dve.wait_ge(back_done, k - 1)
                        nc.vector.tensor_tensor_scan(R[:, b, :], mk[:, s // 2, 1, b * GE:(b + 1) * GE], psM[:, b, :],
                                                     R[:, 1 - b, GE - 1:GE], ALU.add, ALU.max).then_inc(scanned, 1)

                    indices(0, 0)
                    indices(0, 1)

                    def step(i, s):
                        k = GPI * i + s
                        onehot(i, s)
                        if not (isinstance(k, int) and k + 2 >= NGRP):
                            indices(i + (s + 2) // GPI, (s + 2) % GPI)
                        if there(k - 1):
                            scan(k - 1, (s + 3) % GPI)
                    sweep(dve, step)
                    scan(NGRP - 1, GPI - 1)
                    dve.wait_ge(z_done, NGRP)
                    nc.vector.tensor_copy(cnt[:, :], psC[:, 0:P]).then_inc(counted, 1)
        edge_keep.close()
        
        with ExitStack() as ph:
            sb, ps = tensors(ph)
            tri = sb("tri", [P, P], fp32)
            ones = sb("ones", [P, P], fp32)
            cum = sb("cum", [P, P], fp32)
            endf = sb("endf", [P, P], fp32)
            hasc = sb("hasc", [P, P], fp32)
            miss = sb("miss", [P, P], fp32)
            rowI = sb("rowI", [P, P], i32)
            u1 = sb("u1", [P, 2, D], fp32)
            u2 = sb("u2", [P, D], fp32)
            rootw = sb("rootw", [P, D], fp32)
            bas = sb("bas", [P, NB, D], fp32)
            compb = sb("compb", [P, NR, NB], fp32)
            Wr = sb("Wr", [P, NR, D], fp32)
            c1c = sb("c1c", [P, 1], fp32)
            b2b = sb("b2b", [P, D], fp32)
            c2b = sb("c2b", [P, D], fp32)
            biasb = sb("biasb", [P, D], fp32)
            epsd = sb("epsd", [P, 1], fp32)
            lasts = sb("lasts", [P, 2, CH], i32)
            agg = sb("agg", [P, 2, CH, D], fp32)
            aggT = sb("aggT", [P, CW], fp32)
            y1 = sb("y1", [P, CW], fp32)
            endI = aggT[:, 0:4 * P].bitcast(i32).rearrange("p (a n) -> p a n", a=4)
            hn2 = sb("hn2", [P, CH, D], fp32)
            hs2 = sb("hs2", [P, CW], fp32)
            sq2 = sb("sq2", [P, CW], fp32)
            xsum2 = sb("xsum2", [P, CH], fp32)
            xvar2 = sb("xvar2", [P, CH], fp32)
            std2 = sb("std2", [P, CH], fp32)
            rs2 = sb("rs2", [P, CH], fp32)
            pst = sb("pst", [P, 2, CH, NR * D], fp32)
            psA = ps("psA", [P, 1024])
            psY = ps("psY", [P, 1024])
            psX = ps("psX", [P, 1024])
            psP = ps("psP", [P, 2, 512])

            tri_made = sem("tri_made")
            wts_loaded = sem("wts_loaded")
            end_step = sem("end_step")
            ends_off = sem("ends_off")
            last_out = sem("last_out")
            has_out = sem("has_out")
            last_in = sem("last_in")
            has_in = sem("has_in")
            wr_step = sem("wr_step")
            agg_ready = sem("agg_ready")
            agg_got = [sem(f"agg_got{n}") for n in range(2)]
            agg_fixed = sem("agg_fixed")
            aggT_done = sem("aggT_done")
            aggT_copied = sem("aggT_copied")
            y1_done = sem("y1_done")
            y1_relu = sem("y1_relu")
            y2_done = sem("y2_done")
            x1_added = sem("x1_added")
            x1_done = sem("x1_done")
            xsum2_done = sem("xsum2_done")
            centered2 = sem("centered2")
            squared2 = sem("squared2")
            xvar2_done = sem("xvar2_done")
            std2_done = sem("std2_done")
            rs2_done = sem("rs2_done")
            normed2 = sem("normed2")
            h2_transposed = sem("h2_transposed")
            h2_relu = sem("h2_relu")
            root_done = sem("root_done")
            root_kept = sem("root_kept")
            proj_done = sem("proj_done")
            proj_copied = sem("proj_copied")
            proj_stored = [sem(f"proj_stored{n}") for n in range(2)]

            loads = [(u1[:, 0, :], U1[0:D, :]), (u1[:, 1, :], U1[D:2 * D, :]), (u2[:, :], U2), (rootw[:, :], root),
                     (bas[:, :, :], basis.rearrange("b i o -> i b o")),
                     (compb[:, :, :], comp.partition_broadcast(P)), (c1c[:, :], col(c1)),
                     (b2b[:, :], b2.partition_broadcast(P)), (c2b[:, :], c2.partition_broadcast(P)),
                     (biasb[:, :], bias.partition_broadcast(P))]

            with nc.Block() as block:
                @block.sync
                def _(sp):
                    for to, frm in loads:
                        sp.dma_start(to, frm).then_inc(wts_loaded, 16)
                    sp.wait_ge(end_step, 12)
                    sp.dma_start(last_tab, rowI[:, :]).then_inc(last_out, 16)
                    sp.dma_start(has_tab, hasc[:, :]).then_inc(has_out, 16)
                    sp.wait_ge(last_out, 16)
                    sp.wait_ge(has_out, 16)
                    flat = last_tab.rearrange("a b -> (a b)")[0:NP]
                    sp.dma_start(last[:, :], flat.rearrange("(p t) -> p t", p=P)).then_inc(last_in, 16)
                    flat = has_tab.rearrange("a b -> (a b)")[0:NP]
                    sp.dma_start(has[:, :], flat.rearrange("(p t) -> p t", p=P)).then_inc(has_in, 16)

                    def step(i, u):
                        k = 2 * i + u
                        sp.wait_ge(proj_copied, 2 * CH * (k + 1))
                        sp.dma_start(proj_rows[:, bass.ds(k * CH, CH), :], pst[:, u, :, :]).then_inc(proj_stored[u], 16)
                    pairs(sp, step)
                    for u in range(2):
                        sp.wait_ge(proj_stored[u], 16 * (NCH // 2))

                @block.gpsimd
                def _(pool):
                    pool.memset(tri[:, :], 0.0).then_inc(tri_made, 1)
                    pool.wait_ge(tri_made, 1)
                    pool.affine_select(out=tri[:, :], in_=tri[:, :], compare_op=ALU.is_ge, fill=1.0,
                                       base=0, pattern=[[-1, P]], channel_multiplier=1).then_inc(tri_made, 1)

                    def step(i, u):
                        k = 2 * i + u
                        pool.wait_ge(agg_ready, k + 1)
                        pool.nop(nofuse=True)
                        for t in range(CH):
                            pool.indirect_dma_start(agg[:, u, t, :], None, run_tab,
                                                    bass.IndirectOffsetOnAxis(ap=lasts[:, u, t:t + 1], axis=0),
                                                    bounds_check=EP - 1, oob_is_err=False).then_inc(agg_got[u], 16)
                    pairs(pool, step)

                @block.tensor
                def _(pe):
                    pe.wait_ge(tri_made, 2)
                    pe.wait_ge(end_step, 2)
                    nc.tensor.matmul(psA[:, 0:1], tri[:, :], cum[:, P - 1:P], start=True, stop=True).then_inc(ends_off, 1)
                    pe.wait_ge(end_step, 3)
                    pe.wait_ge(wts_loaded, 16 * len(loads))

                    def update(k, u):
                        pe.wait_ge(agg_fixed, k + 1)
                        after(pe, h2_relu, k - 1)
                        for t in range(CH):
                            ins = nc.tensor.transpose(psA[:, t * P:(t + 1) * P], agg[:, u, t, :], ident[:, :])
                        ins.then_inc(aggT_done, 1)
                        after(pe, y1_relu, k)
                        pe.wait_ge(aggT_copied, k + 1)
                        for n, (a, m) in enumerate(((0, 4 * P), (4 * P, CW - 4 * P))):
                            nc.tensor.matmul(psY[:, a:a + m], u1[:, 0, :], hT[:, bass.ds(k * CW + a, m)], start=True, stop=False)
                            ins = nc.tensor.matmul(psY[:, a:a + m], u1[:, 1, :], aggT[:, a:a + m], start=False, stop=True)
                        ins.then_inc(y1_done, 1)
                        pe.wait_ge(y1_relu, k + 1)
                        after(pe, root_kept, k - 1)
                        for t in range(CH):
                            ins = nc.tensor.matmul(psX[:, t * P:(t + 1) * P], y1[:, t * P:(t + 1) * P], u2[:, :],
                                                   start=True, stop=True)
                        ins.then_inc(y2_done, 1)

                    def project(k):
                        pe.wait_ge(normed2, k + 1)
                        if not (isinstance(k, int) and k == NCH - 1):
                            pe.wait_ge(aggT_copied, k + 2)
                        for t in range(CH):
                            ins = nc.tensor.transpose(psA[:, t * P:(t + 1) * P], hn2[:, t, :], ident[:, :])
                        ins.then_inc(h2_transposed, 1)
                        pe.wait_ge(h2_relu, k + 1)
                        for t in range(CH):
                            for a in range(2):
                                n = (k * CH + t) * 2 + a
                                after(pe, proj_copied, n - 1)
                                nc.tensor.matmul(psP[:, a, :], hs2[:, t * P:(t + 1) * P],
                                                 Wr[:, a * NR // 2:(a + 1) * NR // 2, :].rearrange("p r d -> p (r d)"),
                                                 start=True, stop=True).then_inc(proj_done, 1)
                        if not (isinstance(k, int) and k == NCH - 1):
                            pe.wait_ge(x1_added, k + 2)
                        else:
                            pe.wait_ge(root_kept, k)
                        for t in range(CH):
                            ins = nc.tensor.matmul(psX[:, t * P:(t + 1) * P], hs2[:, t * P:(t + 1) * P], rootw[:, :],
                                                   start=True, stop=True)
                        ins.then_inc(root_done, 1)

                    pe.wait_ge(wr_step, 1)

                    def step(i, u):
                        k = 2 * i + u
                        update(k, u)
                        if there(k - 1):
                            project(k - 1)
                    pairs(pe, step)
                    project(NCH - 1)

                @block.scalar
                def _(act):
                    act.wait_ge(wts_loaded, 16 * len(loads))

                    def update(k):
                        act.wait_ge(aggT_done, k + 1)
                        after(act, y1_done, k)
                        nc.scalar.activation(aggT[:, :], psA[:, 0:CW], ACT.Copy).then_inc(aggT_copied, 1)
                        act.wait_ge(y1_done, k + 1)
                        after(act, y2_done, k)
                        nc.scalar.activation(y1[:, :], psY[:, 0:CW], ACT.Relu, bias=c1c[:, 0:1]).then_inc(y1_relu, 1)

                    def square(k):
                        act.wait_ge(centered2, k + 1)
                        after(act, xvar2_done, k)
                        nc.scalar.activation(sq2[:, :], hn2[:, :, :].rearrange("p t d -> p (t d)"), ACT.Square).then_inc(squared2, 1)

                    def deviation(k):
                        act.wait_ge(xvar2_done, k + 1)
                        after(act, rs2_done, k)
                        nc.scalar.activation(std2[:, :], xvar2[:, :], ACT.Sqrt, bias=epsd[:, 0:1], scale=1.0 / D).then_inc(std2_done, 1)

                    def relu(k):
                        act.wait_ge(h2_transposed, k + 1)
                        after(act, root_done, k)
                        nc.scalar.activation(hs2[:, :], psA[:, 0:CW], ACT.Relu).then_inc(h2_relu, 1)

                    def copies(k, u, n):
                        after(act, proj_stored[u], 16 * n)
                        for t in range(CH):
                            for a in range(2):
                                act.wait_ge(proj_done, (k * CH + t) * 2 + a + 1)
                                nc.scalar.activation(pst[:, u, t, a * 512:(a + 1) * 512], psP[:, a, :],
                                                     ACT.Copy).then_inc(proj_copied, 1)

                    def step(i, u):
                        k = 2 * i + u
                        update(k)
                        if there(k - 1):
                            relu(k - 1)
                        square(k)
                        deviation(k)
                        if there(k - 1):
                            copies(k - 1, (u + 1) % 2, i - 1 + u)
                    pairs(act, step)
                    relu(NCH - 1)
                    copies(NCH - 1, 1, NCH // 2 - 1)

                @block.vector
                def _(dve):
                    done = [0]

                    def link(ins):
                        done[0] += 1
                        ins.then_inc(end_step, 1)
                        dve.wait_ge(end_step, done[0])
                    link(nc.vector.memset(ones[:, :], 1.0))
                    link(nc.vector.tensor_tensor_scan(cum[:, :], ones[:, :], cnt[:, :], 0.0, ALU.mult, ALU.add))
                    dve.wait_ge(ends_off, 1)
                    link(nc.vector.tensor_scalar(cum[:, :], cum[:, :], psA[:, 0:1], -1.0, ALU.add, ALU.add))
                    link(nc.vector.tensor_copy(endI[:, 0, :], cum[:, :]))
                    link(nc.vector.tensor_scalar(endI[:, 1, :], endI[:, 0, :], -GE, None, ALU.bitwise_and))
                    link(nc.vector.tensor_scalar(endI[:, 2, :], endI[:, 0, :], P - 1, 2, ALU.bitwise_and, ALU.logical_shift_left))
                    link(nc.vector.tensor_scalar(endI[:, 3, :], endI[:, 0, :], 7, GT - 1, ALU.logical_shift_right, ALU.bitwise_and))
                    link(nc.vector.tensor_tensor(endI[:, 0, :], endI[:, 1, :], endI[:, 2, :], ALU.bitwise_or))
                    link(nc.vector.tensor_tensor(endI[:, 1, :], endI[:, 0, :], endI[:, 3, :], ALU.bitwise_or))
                    nc.vector.tensor_scalar(hasc[:, :], cnt[:, :], 0.0, None, ALU.is_gt)
                    link(nc.vector.tensor_scalar(miss[:, :], cnt[:, :], 0.0, float(NOROW), ALU.is_le, ALU.mult))
                    link(nc.vector.tensor_tensor(endf[:, :], endI[:, 1, :], hasc[:, :], ALU.mult))
                    link(nc.vector.tensor_tensor(rowI[:, :], endf[:, :], miss[:, :], ALU.add))
                    nc.vector.memset(epsd[:, :], EPS)
                    dve.wait_ge(wts_loaded, 16 * len(loads))
                    for b in range(NB):
                        for r in range(NR):
                            if b == 0:
                                ins = nc.vector.tensor_scalar(Wr[:, r, :], bas[:, b, :], compb[:, r, b:b + 1], None, ALU.mult)
                            else:
                                ins = nc.vector.scalar_tensor_tensor(out=Wr[:, r, :], in0=bas[:, b, :], scalar=compb[:, r, b:b + 1],
                                                                     in1=Wr[:, r, :], op0=ALU.mult, op1=ALU.add)
                        link(ins)
                    nc.vector.memset(ones[:, 0:1], 1.0).then_inc(wr_step, 1)
                    dve.wait_ge(last_in, 16)
                    dve.wait_ge(has_in, 16)

                    def ready(k, u):
                        if there(k - 2):
                            dve.wait_ge(aggT_done, k - 1)
                        nc.vector.memset(agg[:, u, :, :], 0.0)
                        nc.vector.tensor_copy(lasts[:, u, :], last[:, bass.ds(k * CH, CH)]).then_inc(agg_ready, 1)

                    def fix(i, u):
                        k = 2 * i + u
                        dve.wait_ge(agg_got[u], 16 * CH * (i + 1))
                        for t in range(CH):
                            ins = nc.vector.scalar_tensor_tensor(out=agg[:, u, t, :], in0=b2b[:, :], scalar=has[:, bass.ds(k * CH + t, 1)],
                                                                 in1=agg[:, u, t, :], op0=ALU.mult, op1=ALU.add)
                        ins.then_inc(agg_fixed, 1)

                    def norm(k):
                        xc = xa[:, bass.ds(k * CH, CH), :]
                        dve.wait_ge(y2_done, k + 1)
                        nc.vector.tensor_tensor(xc, psX[:, 0:CW].rearrange("p (t d) -> p t d", t=CH), xc, ALU.add).then_inc(x1_added, 1)
                        dve.wait_ge(x1_added, k + 1)
                        nc.vector.tensor_tensor(xc, xc, c2b[:, :].unsqueeze(1).to_broadcast([P, CH, D]), ALU.add).then_inc(x1_done, 1)
                        dve.wait_ge(x1_done, k + 1)
                        dve.nop(nofuse=True)
                        nc.vector.tensor_reduce(xsum2[:, :], xc, AX.X, ALU.add).then_inc(xsum2_done, 1)
                        dve.wait_ge(xsum2_done, k + 1)
                        after(dve, h2_transposed, k)
                        nc.vector.scalar_tensor_tensor(out=hn2[:, :, :], in0=xsum2[:, :].unsqueeze(2).to_broadcast([P, CH, D]),
                                                       scalar=-1.0 / D, in1=xc, op0=ALU.mult, op1=ALU.add).then_inc(centered2, 1)

                    def norm_end(k):
                        dve.wait_ge(squared2, k + 1)
                        nc.vector.tensor_reduce(xvar2[:, :], sq2[:, :].rearrange("p (t d) -> p t d", t=CH), AX.X,
                                                ALU.add).then_inc(xvar2_done, 1)
                        dve.wait_ge(std2_done, k + 1)
                        nc.vector.reciprocal(rs2[:, :], std2[:, :]).then_inc(rs2_done, 1)
                        dve.wait_ge(rs2_done, k + 1)
                        nc.vector.tensor_tensor(hn2[:, :, :], hn2[:, :, :], rs2[:, :].unsqueeze(2).to_broadcast([P, CH, D]),
                                                ALU.mult).then_inc(normed2, 1)

                    def root_keep(k):
                        dve.wait_ge(root_done, k + 1)
                        nc.vector.tensor_tensor(hT[:, bass.ds(k * CW, CW)].rearrange("p (t d) -> p t d", t=CH),
                                                psX[:, 0:CW].rearrange("p (t d) -> p t d", t=CH),
                                                biasb[:, :].unsqueeze(1).to_broadcast([P, CH, D]), ALU.add).then_inc(root_kept, 1)

                    ready(0, 0)
                    ready(1, 1)

                    def step(i, u):
                        k = 2 * i + u
                        fix(i, u)
                        norm(k)
                        if not (isinstance(k, int) and k + 2 >= NCH):
                            ready(k + 2, u)
                        norm_end(k)
                        if there(k - 1):
                            root_keep(k - 1)
                    pairs(dve, step)
                    root_keep(NCH - 1)

        with ExitStack() as ph:
            sb, ps = tensors(ph)
            G = sb("G1", [P, GPI, GT, D], fp32)
            R = sb("R1", [P, 2, GE], fp32)
            O = sb("O1", [P, 2, GE], fp32)
            mk = sb("mk1", [P, 2, HALF], bf16)
            idxs = sb("idxs1", [P, GPI, GT], i32)
            psM = ps("psM1", [P, 2, GE])
            psB = ps("psB1", [P, 2, GE])

            idx_ready = sem("l1_idx_ready")
            gathered = [sem(f"l1_gathered{n}") for n in range(GPI)]
            marks_loaded = [sem(f"l1_marks_loaded{n}") for n in range(2)]
            msg_done = sem("l1_msg_done")
            scanned = sem("l1_scanned")
            back_done = sem("l1_back_done")
            back_copied = sem("l1_back_copied")
            stored = [sem(f"l1_stored{n}") for n in range(2)]

            with nc.Block() as block:
                @block.sync
                def _(sp):
                    def step(i, s):
                        k = GPI * i + s
                        if s % 2 == 0:
                            if there(k - GPI):
                                sp.wait_ge(scanned, k - 1)
                            sp.dma_start(mk[:, s // 2, :], marks[2, bass.ds(k * GE, HALF)].partition_broadcast(P)
                                         ).then_inc(marks_loaded[s // 2], 16)
                    sweep(sp, step)

                @block.gpsimd
                def _(pool):
                    def step(i, s):
                        k = GPI * i + s
                        pool.wait_ge(idx_ready, k + 1)
                        pool.nop(nofuse=True)
                        if there(k - GPI):
                            pool.wait_ge(msg_done, k - GPI + 1)
                            pool.nop(nofuse=True)
                        for j in range(GT):
                            pool.indirect_dma_start(G[:, s, j, :], None, proj_tab,
                                                    bass.IndirectOffsetOnAxis(ap=idxs[:, s, j:j + 1], axis=0)
                                                    ).then_inc(gathered[s], 16)
                    sweep(pool, step)

                @block.tensor
                def _(pe):
                    def msg(i, s):
                        k, b = GPI * i + s, s % 2
                        pe.wait_ge(gathered[s], 16 * GT * (i + 1))
                        if there(k - 2):
                            pe.wait_ge(scanned, k)
                        for j in range(GT):
                            ins = nc.tensor.transpose(psM[:, b, j * P:(j + 1) * P], G[:, s, j, :], ident[:, :])
                        ins.then_inc(msg_done, 1)

                    def back(k, b):
                        pe.wait_ge(scanned, k + 2)
                        if there(k - 2):
                            pe.wait_ge(back_copied, k - 1)
                        for j in range(GT):
                            ins = nc.tensor.transpose(psB[:, b, j * P:(j + 1) * P], R[:, b, j * P:(j + 1) * P], ident[:, :])
                        ins.then_inc(back_done, 1)

                    def step(i, s):
                        k = GPI * i + s
                        msg(i, s)
                        if there(k - 1):
                            back(k - 1, (s + 1) % 2)
                    sweep(pe, step)
                    back(NGRP - 1, 1)

                @block.scalar
                def _(act):
                    def put(k, b, n):
                        act.wait_ge(back_done, k + 1)
                        after(act, stored[b], 16 * n)
                        nc.scalar.activation(O[:, b, :], psB[:, b, :], ACT.Copy).then_inc(back_copied, 1)
                        act.wait_ge(back_copied, k + 1)
                        act.dma_start(run_rows[:, bass.ds(k, 1), :].rearrange("p g d -> p (g d)"), O[:, b, :]).then_inc(stored[b], 16)

                    def step(i, s):
                        put(GPI * i + s, s % 2, 2 * i + s // 2)
                    sweep(act, step)
                    for b in range(2):
                        act.wait_ge(stored[b], 16 * (NGRP // 2))

                @block.vector
                def _(dve):
                    nc.vector.memset(R[:, 1, :], 0.0).then_inc(scanned, 1)

                    def indices(i, s):
                        k = GPI * i + s
                        if there(k - GPI):
                            dve.wait_ge(gathered[s], 16 * GT * i)
                        nc.vector.tensor_copy(idxs[:, s, :], idx1[:, bass.ds(k * GT, GT)]).then_inc(idx_ready, 1)

                    def scan(i, s):
                        k, b = GPI * i + s, s % 2
                        dve.wait_ge(marks_loaded[s // 2], 16 * (i + 1))
                        dve.wait_ge(msg_done, k + 1)
                        dve.wait_ge(scanned, k + 1)
                        if there(k - 2):
                            dve.wait_ge(back_done, k - 1)
                        nc.vector.tensor_tensor_scan(R[:, b, :], mk[:, s // 2, b * GE:(b + 1) * GE], psM[:, b, :],
                                                     R[:, 1 - b, GE - 1:GE], ALU.mult, ALU.add).then_inc(scanned, 1)
                    indices(0, 0)
                    indices(0, 1)

                    def step(i, s):
                        k = GPI * i + s
                        if not (isinstance(k, int) and k + 2 >= NGRP):
                            indices(i + (s + 2) // GPI, (s + 2) % GPI)
                        scan(i, s)
                    sweep(dve, step)

        with ExitStack() as ph:
            sb, ps = tensors(ph)
            agg = sb("agg1", [P, 2, CH, D], fp32)
            pre = sb("pre", [P, 2, CH, D], fp32)
            lasts = sb("lasts1", [P, 2, CH], i32)
            agg_ready = sem("l1_agg_ready")
            agg_got = [sem(f"l1_agg_got{n}") for n in range(2)]
            summed = sem("l1_summed")
            relu_done = sem("l1_relu_done")
            x2_done = sem("x2_done")
            out_stored = sem("out_stored")

            with nc.Block() as block:
                @block.gpsimd
                def _(pool):
                    def step(i, u):
                        pool.wait_ge(agg_ready, 2 * i + u + 1)
                        pool.nop(nofuse=True)
                        for t in range(CH):
                            pool.indirect_dma_start(agg[:, u, t, :], None, run_tab,
                                                    bass.IndirectOffsetOnAxis(ap=lasts[:, u, t:t + 1], axis=0),
                                                    bounds_check=EP - 1, oob_is_err=False).then_inc(agg_got[u], 16)
                    pairs(pool, step)

                @block.scalar
                def _(act):
                    def step(i, u):
                        k = 2 * i + u
                        act.wait_ge(summed, k + 1)
                        nc.scalar.activation(pre[:, u, :, :], pre[:, u, :, :], ACT.Relu).then_inc(relu_done, 1)
                    pairs(act, step)

                @block.vector
                def _(dve):
                    def ready(k, u):
                        if there(k - 2):
                            dve.wait_ge(summed, k - 1)
                        nc.vector.memset(agg[:, u, :, :], 0.0)
                        nc.vector.tensor_copy(lasts[:, u, :], last[:, bass.ds(k * CH, CH)]).then_inc(agg_ready, 1)

                    def total(i, u):
                        k = 2 * i + u
                        dve.wait_ge(agg_got[u], 16 * CH * (i + 1))
                        if there(k - 2):
                            dve.wait_ge(x2_done, k - 1)
                        nc.vector.tensor_tensor(pre[:, u, :, :], hT[:, bass.ds(k * CW, CW)].rearrange("p (t d) -> p t d", t=CH),
                                                agg[:, u, :, :], ALU.add).then_inc(summed, 1)

                    def result(k, u):
                        dve.wait_ge(relu_done, k + 1)
                        xc = xa[:, bass.ds(k * CH, CH), :]
                        nc.vector.tensor_tensor(xc, xc, pre[:, u, :, :], ALU.add).then_inc(x2_done, 1)
                    ready(0, 0)
                    ready(1, 1)

                    def step(i, u):
                        k = 2 * i + u
                        total(i, u)
                        if not (isinstance(k, int) and k + 2 >= NCH):
                            ready(k + 2, u)
                        if there(k - 1):
                            result(k - 1, 1 - u)
                    pairs(dve, step)
                    result(NCH - 1, 1)

                @block.sync
                def _(sp):
                    def step(i, u):
                        k = 2 * i + u
                        sp.wait_ge(x2_done, k + 1)
                        sp.dma_start(out_rows[:, bass.ds(k * CH, CH), :], xa[:, bass.ds(k * CH, CH), :]).then_inc(out_stored, 16)
                    pairs(sp, step)
                    sp.wait_ge(out_stored, 16 * NCH)


_INS = ['x', 'dst', 'src_cols', 'dst_cols', 'type_cols', 'w', 'W1', 'b1', 'W2', 'b2', 'U1', 'c1', 'U2', 'c2',
        'basis', 'comp', 'root', 'bias']


def kernel(x, src, dst, edge_type_8, edge_weight, L0_gnn_W1, L0_gnn_b1, L0_gnn_W2, L0_gnn_b2, L0_gnn_U1, L0_gnn_c1,
           L0_gnn_U2, L0_gnn_c2, L1_gnn_weight, L1_gnn_w_comp, L1_gnn_root_weight, L1_gnn_bias):
    import numpy as np
    import concourse.bacc as bacc
    from concourse.bass_utils import run_bass_kernel_spmd as run

    x, src, dst, kind, w = (np.asarray(a) for a in (x, src, dst, edge_type_8, edge_weight))
    n, d = x.shape
    e = src.shape[0]
    n_pad = -(-n // (14 * P)) * 14 * P
    e_pad = -(-e // (TPI * P)) * TPI * P
    assert n < n_pad

    def columns(v, fill):
        return np.ascontiguousarray(np.pad(v, (0, e_pad - e), constant_values=fill).reshape(-1, P).T)

    ins = {
        'x': np.pad(x, ((0, n_pad - n), (0, 0))),
        'dst': np.pad(np.pad(dst, (0, e_pad - e), constant_values=n), (1, 0), constant_values=-1),
        'src_cols': columns(src, 0), 'dst_cols': columns(dst, n), 'type_cols': columns(kind, 0),
        'w': np.pad(w, (0, e_pad - e)),
        'W1': L0_gnn_W1, 'b1': L0_gnn_b1, 'W2': L0_gnn_W2, 'b2': L0_gnn_b2, 'U1': L0_gnn_U1, 'c1': L0_gnn_c1,
        'U2': L0_gnn_U2, 'c2': L0_gnn_c2, 'basis': L1_gnn_weight, 'comp': L1_gnn_w_comp,
        'root': L1_gnn_root_weight, 'bias': L1_gnn_bias}
    nc = bacc.Bacc("TRN2", target_bir_lowering=False, num_devices=1)
    arrays, args = {}, []
    for name in _INS:
        a = np.ascontiguousarray(ins[name])
        arrays[f"in_{name}"] = a
        args.append(nc.dram_tensor(f"in_{name}", a.shape, mybir.dt.from_np(a.dtype), kind="ExternalInput").ap())
    args.append(nc.dram_tensor("out_x", (n_pad, d), mybir.dt.float32, kind="ExternalOutput").ap())
    gnn(nc, *args)
    r = run(nc, [arrays], core_ids=[0])
    return r.results[0]["out_x"][:n]
```

```python
import concourse.bass as bass
from concourse import mybir
from contextlib import ExitStack

P = 128
GT = 4
GE = GT * P
GPI = 4
TPI = GT * GPI
LOGW = 6
W = 1 << LOGW


def after(eng, sem, n):
    if not (isinstance(n, int) and n <= 0):
        eng.wait_ge(sem, n)


def there(k):
    return not (isinstance(k, int) and k < 0)


def gnn(nc, x, dst, first, last, src_cols, dst_cols, next_cols, type_cols, w, W1, b1, W2, b2, U1, c1, U2, c2,
        basis, comp_t, root, bias, out, n_real):
    fp32, bf16, i32 = mybir.dt.float32, mybir.dt.bfloat16, mybir.dt.int32
    ALU, ACT, AX = mybir.AluOpType, mybir.ActivationFunctionType, mybir.AxisListType
    RMAX = bass.bass_isa.ReduceOp.max

    NP, D = x.shape
    NT = NP // P
    ET = src_cols.shape[1]
    EP = ET * P
    ITERS = ET // TPI
    NGRP = ITERS * GPI
    NB, _, _ = basis.shape
    NR = comp_t.shape[1]
    CH = 7
    NCH = NT // CH
    CW = CH * P
    CA = 4 * P
    MP = 112
    MG = NGRP // MP
    HALF = 2 * GE
    EPS = 1e-5
    LOW = 3.0e38
    FAR = 2.0 ** 20
    assert NT % (2 * CH) == 0 and 7 * MG * GE // 2 <= NP and NGRP % MP == 0 and D == P and ITERS >= 3

    p_tab = nc.dram_tensor("p_tab", (NP, D), fp32).ap()
    q_tab = nc.dram_tensor("q_tab", (NP + W, D), fp32).ap()
    h2_tab = nc.dram_tensor("h2_tab", (NP, D), fp32).ap()
    marks = nc.dram_tensor("marks", (2, EP), bf16).ap()
    relc_tab = nc.dram_tensor("relc_tab", (P, ET), bf16).ap()

    p_rows = p_tab.rearrange("(t p) d -> p t d", p=P)
    q_rows = q_tab[0:NP, :].rearrange("(t p) d -> p t d", p=P)
    h2_rows = h2_tab.rearrange("(t p) d -> p t d", p=P)
    x_rows = x.rearrange("(t p) d -> p t d", p=P)
    out_rows = out.rearrange("(t p) d -> p t d", p=P)

    ctx = ExitStack()

    def sem(name):
        return ctx.enter_context(nc.semaphore(name))

    def tensors(stack, tag=""):
        def sb(name, shape, dt):
            return stack.enter_context(nc.sbuf_tensor(name + tag, shape, dt))

        def ps(name, shape):
            return stack.enter_context(nc.psum_tensor(name + tag, shape, fp32))
        return sb, ps

    def row(v):
        return v.rearrange("(a n) -> a n", a=1)

    def col(v):
        return v.rearrange("(n a) -> n a", a=1)

    def flat(v):
        return v.rearrange("p a d -> p (a d)")

    def pairs(eng, step):
        for u in range(2):
            step(0, u)
        with eng.Fori(1, NCH // 2 - 1) as i:
            for u in range(2):
                step(i, u)
        for u in range(2):
            step(NCH // 2 - 1, u)

    def sweep(eng, step):
        for s in range(GPI):
            step(0, s)
        with eng.Fori(1, ITERS - 1) as i:
            for s in range(GPI):
                step(i, s)
        for s in range(GPI):
            step(ITERS - 1, s)

    def marks_memory(work):
        n = MG * GE
        dI, pI = work[:, 0:n].bitcast(i32), work[:, n:2 * n].bitcast(i32)
        b16 = work[:, 2 * n:2 * n + 3 * n // 2].bitcast(bf16)
        return dI, pI, b16[:, 0:n], b16[:, n:2 * n], b16[:, 2 * n:3 * n]

    def marks_sync(sp, m, base_b):
        dI, pI, cont, lowm, relb = m
        sp.dma_start(dI[0:MP, :], dst[1:EP + 1].rearrange("(p e) -> p e", p=MP)).then_inc(dst_loaded, 16)
        sp.dma_start(pI[0:MP, :], dst[0:EP].rearrange("(p e) -> p e", p=MP)).then_inc(prev_loaded, 16)
        sp.dma_start(base_b[:, :], first.partition_broadcast(P)).then_inc(base_loaded, 16)

    def marks_sync_end(sp, m, relc, wide=False):
        dI, pI, cont, lowm, relb = m
        sp.wait_ge(mark_step, 4 if wide else 3)
        sp.dma_start(marks[0, :].rearrange("(p e) -> p e", p=MP), relb[0:MP, :]).then_inc(marks_stored, 16)
        sp.dma_start(marks[1, :].rearrange("(p e) -> p e", p=MP), lowm[0:MP, :]).then_inc(marks_stored, 16)
        sp.wait_ge(extent_ready, 2)
        sp.dma_start(dI[:, 0:ET], dst_cols).then_inc(cols_loaded, 16)
        sp.dma_start(pI[:, 0:ET], next_cols).then_inc(next_loaded, 16)
        sp.wait_ge(cols_step, 4)
        sp.dma_start(relc_tab, relc).then_inc(relc_stored, 16)
        sp.wait_ge(marks_stored, 32)
        sp.wait_ge(relc_stored, 16)

    def marks_vector(dve, m, ext, wide=False):
        dI, pI, cont, lowm, relb = (v[0:MP, :] for v in m)
        g3 = lambda v: v.rearrange("p (g e) -> p g e", e=GE)
        base = g3(dI)[:, :, 0:1].to_broadcast([MP, MG, GE])
        dve.wait_ge(dst_loaded, 16)
        dve.wait_ge(prev_loaded, 16)
        nc.vector.tensor_tensor(cont, dI, pI, ALU.is_equal).then_inc(mark_step, 1)
        dve.wait_ge(mark_step, 1)
        nc.vector.tensor_scalar(lowm, cont, -1.0, LOW, ALU.add, ALU.mult).then_inc(mark_step, 1)
        dve.wait_ge(shift_set, 1)
        nc.vector.scalar_tensor_tensor(out=g3(relb), in0=g3(dI), scalar=shift[0:MP, 0:1], in1=base,
                                       op0=ALU.add, op1=ALU.subtract).then_inc(mark_step, 1)
        if wide:
            last = g3(dI)[:, :, GE - 1:GE].to_broadcast([MP, MG, GE])
            nc.vector.tensor_tensor(g3(cont), g3(dI), last, ALU.not_equal).then_inc(wide_step, 1)
            dve.wait_ge(wide_step, 1)
            nc.vector.tensor_scalar(cont, cont, FAR, W - 0.5, ALU.mult, ALU.add).then_inc(wide_step, 1)
            dve.wait_ge(wide_step, 2)
            dve.wait_ge(mark_step, 3)
            nc.vector.tensor_tensor(relb, relb, cont, ALU.min).then_inc(mark_step, 1)
        span = pI.bitcast(fp32)
        dve.wait_ge(mark_step, 2)
        nc.vector.tensor_tensor(g3(span), g3(dI), base, ALU.subtract).then_inc(span_step, 1)
        dve.wait_ge(span_step, 1)
        nc.vector.scalar_tensor_tensor(out=span, in0=dI, scalar=float(n_real), in1=span,
                                       op0=ALU.is_lt, op1=ALU.mult).then_inc(span_step, 1)
        dve.wait_ge(span_step, 2)
        dve.wait_ge(extent_ready, 1)
        nc.vector.tensor_reduce(ext[0:MP, 0:1], span, AX.X, ALU.max).then_inc(extent_ready, 1)

    def marks_vector_cols(dve, m, base_b, relc, relL):
        dcol, ncol = m[0][:, 0:ET], m[1][:, 0:ET]
        islast = m[2][:, 0:ET]
        g3 = lambda v: v.rearrange("p (g t) -> p g t", t=GT)
        dve.wait_ge(cols_loaded, 16)
        dve.wait_ge(next_loaded, 16)
        dve.wait_ge(base_loaded, 16)
        nc.vector.tensor_tensor(islast, dcol, ncol, ALU.not_equal).then_inc(cols_step, 1)
        nc.vector.scalar_tensor_tensor(out=g3(relc), in0=g3(dcol), scalar=shift[:, 0:1],
                                       in1=base_b[:, :].unsqueeze(2).to_broadcast([P, NGRP, GT]),
                                       op0=ALU.add, op1=ALU.subtract).then_inc(cols_step, 1)
        dve.wait_ge(cols_step, 2)
        nc.vector.scalar_tensor_tensor(out=relL[:, :], in0=relc, scalar=1.0, in1=islast,
                                       op0=ALU.add, op1=ALU.mult).then_inc(cols_step, 1)
        dve.wait_ge(cols_step, 3)
        nc.vector.tensor_scalar(relL[:, :], relL[:, :], -1.0, None, ALU.add).then_inc(cols_step, 1)
        dve.wait_ge(cols_step, 4)

    with ctx:
        keep, _ = tensors(ctx)
        aggT = keep("aggT", [P, NP + W], fp32)
        ident = keep("ident", [P, P], fp32)
        idx0 = keep("idx0", [P, ET], i32)
        win = keep("win", [1, NGRP], i32)
        lane = keep("lane", [P, W], fp32)
        pidx = keep("pidx", [P, 1], fp32)
        shift = keep("shift", [P, 1], fp32)
        npass = keep("npass", [1, 1], i32)
        work = aggT

        dst_loaded = sem("dst_loaded")
        prev_loaded = sem("prev_loaded")
        base_loaded = sem("base_loaded")
        cols_loaded = sem("cols_loaded")
        next_loaded = sem("next_loaded")
        mark_step = sem("mark_step")
        span_step = sem("span_step")
        cols_step = sem("cols_step")
        extent_ready = sem("extent_ready")
        marks_stored = sem("marks_stored")
        relc_stored = sem("relc_stored")
        shift_set = sem("shift_set")
        wide_step = sem("wide_step")
        mark_sems = [dst_loaded, prev_loaded, base_loaded, cols_loaded, next_loaded, mark_step, span_step, cols_step,
                     extent_ready, marks_stored, relc_stored, shift_set, wide_step]

        hstack = ctx.enter_context(ExitStack())
        hkeep, _ = tensors(hstack)
        hT = hkeep("hT", [P, NT * P], fp32)
        estack = ctx.enter_context(ExitStack())
        ekeep, _ = tensors(estack)
        relL = ekeep("relL", [P, ET], bf16)
        with ExitStack() as ph:
            sb, ps = tensors(ph)
            xa = sb("xa0", [P, NT, D], fp32)
            w1ab = sb("w1ab", [P, 2, D], fp32)
            xsum = sb("xsum", [P, 2, CH], fp32)
            xvar = sb("xvar", [P, 2, CH], fp32)
            std = sb("std", [P, 2, CH], fp32)
            rstd = sb("rstd", [P, 2, CH], fp32)
            epsc = sb("epsc", [P, 1], fp32)
            hn = sb("hn", [P, 2, CH, D], fp32)
            hs = sb("hs", [P, CW], fp32)
            pq = sb("pq", [P, CH, 2, D], fp32)
            relc = sb("relc", [P, ET], bf16)
            base_b = sb("base_b", [P, NGRP], i32)
            ext = sb("ext", [P, 1], fp32)
            exta = sb("exta", [P, 1], fp32)
            extI = sb("extI", [P, 2], i32)
            zrow = sb("zrow", [W, D], fp32)
            m = marks_memory(work[:, :])
            psH = ps("psH", [P, 1024])
            psQ = ps("psQ", [P, 2048])
            psS = ps("psS", [P, 1024])

            x_loaded = sem("x_loaded")
            w1_loaded = sem("w1_loaded")
            idx_loaded = sem("idx_loaded")
            pad_zeroed = sem("pad_zeroed")
            ident_zeroed = sem("ident_zeroed")
            ident_ready = sem("ident_ready")
            iota_ready = sem("iota_ready")
            eps_ready = sem("eps_ready")
            xsum_done = sem("xsum_done")
            centered = sem("centered")
            squared = sem("squared")
            xvar_done = sem("xvar_done")
            std_done = sem("std_done")
            rstd_done = sem("rstd_done")
            normed = sem("normed")
            h_transposed = sem("h_transposed")
            h_relu = sem("h_relu")
            h_kept = sem("h_kept")
            pq_done = sem("pq_done")
            pq_copied_a = sem("pq_copied_a")
            pq_copied_b = sem("pq_copied_b")
            p_stored = sem("p_stored")
            q_stored = sem("q_stored")
            extent_joined = sem("extent_joined")
            pass_step = sem("pass_step")
            pad_stored = sem("pad_stored")
            win_loaded = sem("win_loaded")

            with nc.Block() as block:
                @block.sync
                def _(sp):
                    for a in range(2):
                        sp.dma_start(w1ab[:, a, :], W1[a * D:(a + 1) * D, :]).then_inc(w1_loaded, 16)
                        sp.wait_ge(w1_loaded, 16 * (a + 1))
                    sp.dma_start(xa[:, :, :], x_rows).then_inc(x_loaded, 16)
                    sp.dma_start(idx0[:, :], src_cols).then_inc(idx_loaded, 16)
                    sp.dma_start(win[:, :], row(first)).then_inc(win_loaded, 16)
                    marks_sync(sp, m, base_b)

                    def store(c):
                        sp.wait_ge(pq_copied_a, c + 1)
                        sp.wait_ge(pq_copied_b, c + 1)
                        sp.dma_start(p_rows[:, bass.ds(c * CH, CH), :], pq[:, :, 0, :]).then_inc(p_stored, 16)
                        sp.dma_start(q_rows[:, bass.ds(c * CH, CH), :], pq[:, :, 1, :]).then_inc(q_stored, 16)
                    with sp.Fori(0, NCH) as c:
                        store(c)
                    sp.wait_ge(pad_zeroed, 1)
                    sp.dma_start(q_tab[NP:NP + W, :], zrow[:, :]).then_inc(pad_stored, 16)
                    marks_sync_end(sp, m, relc[:, :])
                    sp.wait_ge(p_stored, 16 * NCH)
                    sp.wait_ge(q_stored, 16 * NCH)
                    sp.wait_ge(pad_stored, 16)
                    sp.wait_ge(idx_loaded, 16)
                    sp.wait_ge(win_loaded, 16)

                @block.gpsimd
                def _(pool):
                    pool.memset(ident[:, :], 0.0).then_inc(ident_zeroed, 1)
                    pool.wait_ge(ident_zeroed, 1)
                    pool.affine_select(out=ident[:, :], in_=ident[:, :], compare_op=ALU.not_equal, fill=1.0,
                                       base=0, pattern=[[-1, P]], channel_multiplier=1).then_inc(ident_ready, 1)
                    pool.iota(lane[:, :], pattern=[[1, W]], base=0, channel_multiplier=0,
                              allow_small_or_imprecise_dtypes=True)
                    pool.iota(pidx[:, :], pattern=[[0, 1]], base=0, channel_multiplier=1,
                              allow_small_or_imprecise_dtypes=True)
                    pool.memset(shift[:, :], 0.0).then_inc(shift_set, 1)
                    pool.memset(zrow[:, :], 0.0).then_inc(pad_zeroed, 1)
                    pool.wait_ge(extent_ready, 2)
                    pool.partition_all_reduce(exta[:, :], ext[:, :], P, RMAX).then_inc(extent_joined, 1)

                @block.scalar
                def _(act):
                    act.wait_ge(eps_ready, 1)

                    def square(k, u):
                        act.wait_ge(centered, k + 1)
                        after(act, xvar_done, k)
                        nc.scalar.activation(psS[:, 0:CW], hn[:, u, :, :].rearrange("p t d -> p (t d)"), ACT.Square).then_inc(squared, 1)

                    def deviation(k, u):
                        act.wait_ge(xvar_done, k + 1)
                        nc.scalar.activation(std[:, u, :], xvar[:, u, :], ACT.Sqrt, bias=epsc[:, 0:1], scale=1.0 / D).then_inc(std_done, 1)

                    def relu(k):
                        act.wait_ge(h_transposed, k + 1)
                        after(act, pq_done, k)
                        nc.scalar.activation(hs[:, :], psH[:, 0:CW], ACT.Relu).then_inc(h_relu, 1)
                        nc.scalar.activation(hT[:, bass.ds(k * CW, CW)], psH[:, 0:CW], ACT.Relu).then_inc(h_kept, 1)

                    def copy_pq(k):
                        act.wait_ge(pq_done, k + 1)
                        after(act, p_stored, k * 16)
                        after(act, q_stored, k * 16)
                        nc.scalar.activation(pq[:, 0:4, :, :].rearrange("p t a d -> p (t a d)"), psQ[:, 0:1024],
                                             ACT.Copy).then_inc(pq_copied_a, 1)
                    square(0, 0)

                    def step(i, u):
                        k = 2 * i + u
                        if not (isinstance(k, int) and k + 1 >= NCH):
                            square(k + 1, 1 - u)
                        deviation(k, u)
                        if there(k - 1):
                            copy_pq(k - 1)
                        relu(k)
                    pairs(act, step)
                    copy_pq(NCH - 1)

                @block.tensor
                def _(pe):
                    pe.wait_ge(ident_ready, 1)
                    pe.wait_ge(w1_loaded, 32)

                    def step(i, u):
                        k = 2 * i + u
                        pe.wait_ge(normed, k + 1)
                        after(pe, h_kept, k)
                        for t in range(CH):
                            ins = nc.tensor.transpose(psH[:, t * P:(t + 1) * P], hn[:, u, t, :], ident[:, :])
                        ins.then_inc(h_transposed, 1)
                        pe.wait_ge(h_relu, k + 1)
                        after(pe, pq_copied_a, k)
                        after(pe, pq_copied_b, k)
                        for t in range(CH):
                            ins = nc.tensor.matmul(psQ[:, t * 2 * D:(t + 1) * 2 * D], hs[:, t * P:(t + 1) * P],
                                                   w1ab[:, :, :].rearrange("p a d -> p (a d)"), start=True, stop=True)
                        ins.then_inc(pq_done, 1)
                    pairs(pe, step)

                @block.vector
                def _(dve):
                    nc.vector.memset(epsc[:, :], EPS).then_inc(eps_ready, 1)
                    nc.vector.memset(ext[:, :], 0.0).then_inc(extent_ready, 1)
                    dve.wait_ge(x_loaded, 16)

                    def center(k, u):
                        xc = xa[:, bass.ds(k * CH, CH), :]
                        nc.vector.tensor_reduce(xsum[:, u, :], xc, AX.X, ALU.add).then_inc(xsum_done, 1)
                        dve.wait_ge(xsum_done, k + 1)
                        if there(k - 2):
                            dve.wait_ge(h_transposed, k - 1)
                        nc.vector.scalar_tensor_tensor(out=hn[:, u, :, :], in0=xsum[:, u, :].unsqueeze(2).to_broadcast([P, CH, D]),
                                                       scalar=-1.0 / D, in1=xc, op0=ALU.mult, op1=ALU.add).then_inc(centered, 1)

                    def scale(k, u):
                        dve.wait_ge(std_done, k + 1)
                        nc.vector.reciprocal(rstd[:, u, :], std[:, u, :]).then_inc(rstd_done, 1)
                        dve.wait_ge(rstd_done, k + 1)
                        nc.vector.tensor_tensor(hn[:, u, :, :], hn[:, u, :, :], rstd[:, u, :].unsqueeze(2).to_broadcast([P, CH, D]),
                                                ALU.mult).then_inc(normed, 1)

                    def variance(k, u):
                        dve.wait_ge(squared, k + 1)
                        nc.vector.tensor_reduce(xvar[:, u, :], psS[:, 0:CW].rearrange("p (t d) -> p t d", t=CH), AX.X,
                                                ALU.add).then_inc(xvar_done, 1)

                    def copy_pq(k):
                        dve.wait_ge(pq_done, k + 1)
                        after(dve, p_stored, k * 16)
                        after(dve, q_stored, k * 16)
                        nc.vector.tensor_copy(pq[:, 4:CH, :, :].rearrange("p t a d -> p (t a d)"),
                                              psQ[:, 1024:CH * 2 * D]).then_inc(pq_copied_b, 1)
                    center(0, 0)

                    def step(i, u):
                        k = 2 * i + u
                        variance(k, u)
                        if not (isinstance(k, int) and k + 1 >= NCH):
                            dve.nop(nofuse=True)
                            center(k + 1, 1 - u)
                        scale(k, u)
                        if there(k - 1):
                            copy_pq(k - 1)
                    pairs(dve, step)
                    copy_pq(NCH - 1)

                    marks_vector(dve, m, ext)
                    marks_vector_cols(dve, m, base_b, relc[:, :], relL)
                    dve.wait_ge(extent_joined, 1)
                    nc.vector.tensor_copy(extI[:, 0:1], exta[:, :]).then_inc(pass_step, 1)
                    dve.wait_ge(pass_step, 1)
                    nc.vector.tensor_scalar(extI[:, 1:2], extI[:, 0:1], LOGW, None, ALU.logical_shift_right).then_inc(pass_step, 1)
                    dve.wait_ge(pass_step, 2)
                    nc.vector.tensor_scalar(npass[0:1, 0:1], extI[0:1, 1:2], 1.0, None, ALU.add).then_inc(pass_step, 1)
                    dve.wait_ge(pass_step, 3)

        consts_loaded = sem("consts_loaded")
        w1c_loaded = sem("w1c_loaded")
        agg_zeroed = sem("agg_zeroed")
        idx_ready = sem("idx_ready")
        gathered = [sem(f"gathered{n}") for n in range(GPI)]
        qwin_loaded = [sem(f"qwin_loaded{n}") for n in range(GPI)]
        places_loaded = [sem(f"places_loaded{n}") for n in range(2)]
        masks_loaded = [sem(f"masks_loaded{n}") for n in range(2)]
        wgt_loaded = [sem(f"wgt_loaded{n}") for n in range(2)]
        onehot_ready = sem("onehot_ready")
        z_done = sem("z_done")
        relu_done = sem("relu_done")
        msg_done = sem("msg_done")
        scanned = sem("scanned")
        back_done = sem("back_done")
        picks_ready = sem("picks_ready")
        picked = sem("picked")
        added = sem("added")
        tail_loaded = sem("tail_loaded")
        place_ready = sem("place_ready")
        edge_sems = [tail_loaded, place_ready, consts_loaded, w1c_loaded, agg_zeroed, idx_ready, *gathered, *qwin_loaded, *places_loaded,
                     *masks_loaded, *wgt_loaded, onehot_ready, z_done, relu_done, msg_done, scanned, back_done,
                     picks_ready, picked, added]

        def clear(sems):
            with nc.Block() as block:
                @block.gpsimd
                def _(pool):
                    for s in sems:
                        pool.sem_clear(s)

        def max_edges(tag, again, wide=False):
            WQ = W + wide
            with ExitStack() as ph:
                sb, ps = tensors(ph, tag)
                G = sb("G", [P, GPI, GT, D], fp32)
                Qw = sb("Qw", [WQ + 1, GPI, D], fp32)
                oh = sb("oh", [WQ + 1, GPI, GE], fp32)
                Z = sb("Z", [P, 2, GE], fp32)
                R = sb("R", [P, 2, GE], fp32)
                O = sb("O", [P, 2, GE], fp32)
                E = sb("E", [P, 2, GT, W], fp32)
                pl = sb("pl", [WQ, 2, HALF], bf16)
                mk = sb("mk", [P, 2, HALF], bf16)
                idxs = sb("idxs", [P, GPI, GT], i32)
                w2 = sb("w2", [P, D], fp32)
                b1c = sb("b1c", [P, 1], fp32)
                b2b = sb("b2b", [P, D], fp32)
                place = sb("place", [P, 1], fp32)
                if wide:
                    tail = sb("tail", [1, NGRP], i32)
                psZ = ps("psZ", [P, 2, GE])
                psM = ps("psM", [P, 2, GE])
                psB = ps("psB", [P, 2, GE])
                psE = ps("psE", [P, 2, GE])

                with nc.Block() as block:
                    @block.sync
                    def _(sp):
                        for s in range(GPI):
                            sp.dma_start(Qw[WQ:WQ + 1, s, :], W1[2 * D:2 * D + 1, :]).then_inc(w1c_loaded, 16)
                        sp.dma_start(w2[:, :], W2).then_inc(consts_loaded, 16)
                        sp.dma_start(b1c[:, :], col(b1)).then_inc(consts_loaded, 16)
                        sp.dma_start(b2b[:, :], b2.partition_broadcast(P)).then_inc(consts_loaded, 16)

                        if wide:
                            sp.dma_start(tail[:, :], row(last)).then_inc(tail_loaded, 16)
                            sp.wait_ge(tail_loaded, 16)

                        def step(i, s):
                            k = GPI * i + s
                            if there(k - GPI):
                                sp.wait_ge(z_done, k - GPI + 1 + (s % 2 == 0))
                            sp.nop(nofuse=True)
                            r0 = sp.value_load(win[0:1, bass.ds(k, 1)], min_val=0, max_val=NP)
                            sp.dma_start(Qw[0:W, s, :], q_tab[bass.ds(r0, W), :]).then_inc(qwin_loaded[s], 16)
                            if wide:
                                r1 = sp.value_load(tail[0:1, bass.ds(k, 1)], min_val=0, max_val=NP)
                                sp.dma_start(Qw[W:WQ, s, :], q_tab[bass.ds(r1, 1), :]).then_inc(qwin_loaded[s], 16)
                            if s % 2 == 0:
                                h = s // 2
                                sp.dma_start(oh[WQ:WQ + 1, s:s + 2, :].rearrange("p a e -> p (a e)"),
                                             row(w)[:, bass.ds(k * GE, HALF)]).then_inc(wgt_loaded[h], 16)
                                if there(k - GPI):
                                    sp.wait_ge(scanned, k - 1)
                                    sp.nop(nofuse=True)
                                sp.dma_start(pl[:, h, :], marks[0, bass.ds(k * GE, HALF)].partition_broadcast(WQ)
                                             ).then_inc(places_loaded[h], 16)
                                sp.dma_start(mk[:, h, :], marks[1, bass.ds(k * GE, HALF)].partition_broadcast(P)
                                             ).then_inc(masks_loaded[h], 16)
                        sweep(sp, step)

                    @block.gpsimd
                    def _(pool):
                        def step(i, s):
                            k = GPI * i + s
                            pool.wait_ge(idx_ready, k + 1)
                            pool.nop(nofuse=True)
                            if there(k - GPI):
                                pool.wait_ge(z_done, k - GPI + 1)
                                pool.nop(nofuse=True)
                            for j in range(GT):
                                pool.indirect_dma_start(G[:, s, j, :], None, p_tab,
                                                        bass.IndirectOffsetOnAxis(ap=idxs[:, s, j:j + 1], axis=0)
                                                        ).then_inc(gathered[s], 16)
                        sweep(pool, step)

                    @block.tensor
                    def _(pe):
                        pe.wait_ge(consts_loaded, 48)
                        pe.wait_ge(w1c_loaded, 16 * GPI)

                        def z(i, s):
                            k, b = GPI * i + s, s % 2
                            if there(k - 2):
                                pe.wait_ge(relu_done, k - 1)
                            pe.wait_ge(gathered[s], 16 * GT * (i + 1))
                            for j in range(GT):
                                nc.tensor.matmul(psZ[:, b, j * P:(j + 1) * P], G[:, s, j, :], ident[:, :], is_transpose=True,
                                                 start=j == 0, stop=False)
                            pe.wait_ge(onehot_ready, k + 1)
                            pe.wait_ge(wgt_loaded[s // 2], 16 * (i + 1))
                            pe.wait_ge(qwin_loaded[s], (16 + 16 * wide) * (i + 1))
                            nc.tensor.matmul(psZ[:, b, :], Qw[:, s, :], oh[:, s, :], start=False, stop=True).then_inc(z_done, 1)

                        def msg(k, b):
                            pe.wait_ge(relu_done, k + 1)
                            if there(k - 2):
                                pe.wait_ge(scanned, k)
                            nc.tensor.matmul(psM[:, b, :], w2[:, :], Z[:, b, :], start=True, stop=True).then_inc(msg_done, 1)

                        def back(k, b):
                            pe.wait_ge(scanned, k + 2)
                            if there(k - 2):
                                pe.wait_ge(picks_ready, k - 1)
                            for j in range(GT):
                                ins = nc.tensor.transpose(psB[:, b, j * P:(j + 1) * P], R[:, b, j * P:(j + 1) * P], ident[:, :])
                            ins.then_inc(back_done, 1)

                        def pick(k, b):
                            pe.wait_ge(picks_ready, k + 1)
                            if there(k - 2):
                                pe.wait_ge(added, k - 1)
                            for j in range(GT):
                                ins = nc.tensor.matmul(psE[:, b, 0:W], O[:, b, j * P:(j + 1) * P], E[:, b, j, :],
                                                       start=j == 0, stop=j == GT - 1)
                            ins.then_inc(picked, 1)

                        def step(i, s):
                            k = GPI * i + s
                            z(i, s)
                            if there(k - 1):
                                msg(k - 1, (s + 1) % 2)
                            if there(k - 2):
                                back(k - 2, s % 2)
                            if there(k - 3):
                                pick(k - 3, (s + 1) % 2)
                        sweep(pe, step)
                        msg(NGRP - 1, 1)
                        back(NGRP - 2, 0)
                        pick(NGRP - 3, 1)
                        back(NGRP - 1, 1)
                        pick(NGRP - 2, 0)
                        pick(NGRP - 1, 1)

                    @block.scalar
                    def _(act):
                        act.wait_ge(consts_loaded, 48)

                        def step(i, s):
                            k, b = GPI * i + s, s % 2
                            act.wait_ge(z_done, k + 1)
                            if there(k - 2):
                                act.wait_ge(msg_done, k - 1)
                            nc.scalar.activation(Z[:, b, :], psZ[:, b, :], ACT.Relu, bias=b1c[:, 0:1]).then_inc(relu_done, 1)
                        sweep(act, step)

                    @block.vector
                    def _(dve):
                        nc.vector.tensor_scalar(place[:, :], pidx[:, :], W - 0.5, None, ALU.min).then_inc(place_ready, 1)
                        nc.vector.memset(R[:, 1, :], 0.0).then_inc(scanned, 1)
                        if not again:
                            nc.vector.memset(aggT[:, 0:NP + W], 0.0).then_inc(agg_zeroed, 1)
                            dve.wait_ge(agg_zeroed, 1)
                        dve.wait_ge(consts_loaded, 48)
                        dve.wait_ge(place_ready, 1)

                        def indices(i, s):
                            k = GPI * i + s
                            if there(k - GPI):
                                dve.wait_ge(gathered[s], 16 * GT * i)
                            nc.vector.tensor_copy(idxs[:, s, :], idx0[:, bass.ds(k * GT, GT)]).then_inc(idx_ready, 1)

                        def onehot(i, s):
                            k, b = GPI * i + s, s % 2
                            if there(k - GPI):
                                dve.wait_ge(z_done, k - GPI + 1)
                            dve.wait_ge(places_loaded[s // 2], 16 * (i + 1))
                            nc.vector.tensor_scalar(oh[0:WQ, s, :], pl[:, s // 2, b * GE:(b + 1) * GE], place[0:WQ, 0:1], None,
                                                    ALU.is_equal).then_inc(onehot_ready, 1)

                        def scan(i, s):
                            k, b = GPI * i + s, s % 2
                            dve.wait_ge(masks_loaded[s // 2], 16 * (i + 1))
                            dve.wait_ge(msg_done, k + 1)
                            dve.wait_ge(scanned, k + 1)
                            if there(k - 2):
                                dve.wait_ge(back_done, k - 1)
                            nc.vector.tensor_tensor_scan(R[:, b, :], mk[:, s // 2, b * GE:(b + 1) * GE], psM[:, b, :],
                                                         R[:, 1 - b, GE - 1:GE], ALU.add, ALU.max).then_inc(scanned, 1)

                        def picks(k, b):
                            dve.wait_ge(back_done, k + 1)
                            if there(k - 2):
                                dve.wait_ge(picked, k - 1)
                            nc.vector.tensor_tensor(O[:, b, :].rearrange("p (j d) -> p j d", j=GT),
                                                    psB[:, b, :].rearrange("p (j d) -> p j d", j=GT),
                                                    b2b[:, :].unsqueeze(1).to_broadcast([P, GT, D]), ALU.add)
                            nc.vector.tensor_tensor(E[:, b, :, :], lane[:, :].unsqueeze(1).to_broadcast([P, GT, W]),
                                                    relL[:, bass.ds(k * GT, GT)].unsqueeze(2).to_broadcast([P, GT, W]),
                                                    ALU.is_equal).then_inc(picks_ready, 1)

                        def add(k, b):
                            dve.wait_ge(picked, k + 1)
                            after(dve, added, k)
                            dve.nop(nofuse=True)
                            r0 = dve.value_load(win[0:1, bass.ds(k, 1)], min_val=0, max_val=NP)
                            to = aggT[:, bass.ds(r0, W)]
                            nc.vector.tensor_tensor(to, psE[:, b, 0:W], to, ALU.add).then_inc(added, 1)

                        indices(0, 0)
                        indices(0, 1)

                        def step(i, s):
                            k = GPI * i + s
                            onehot(i, s)
                            if not (isinstance(k, int) and k + 2 >= NGRP):
                                indices(i + (s + 2) // GPI, (s + 2) % GPI)
                            if there(k - 1):
                                scan(i - (s == 0), (s + 3) % GPI)
                            if there(k - 2):
                                picks(k - 2, s % 2)
                            if there(k - 3):
                                add(k - 3, (s + 1) % 2)
                        sweep(dve, step)
                        scan(ITERS - 1, GPI - 1)
                        picks(NGRP - 2, 0)
                        add(NGRP - 3, 1)
                        picks(NGRP - 1, 1)
                        add(NGRP - 2, 0)
                        add(NGRP - 1, 1)

        win_moved = sem("win_moved")

        def move_windows(tag, relL=None, wide=False):
            with ExitStack() as ph:
                sb, _ = tensors(ph, tag)
                if relL is None:
                    spare = hT
                    relL = sb("relLm", [P, ET], bf16)
                else:
                    spare = sb("spare", [P, 7 * MG * GE // 2], fp32)
                relc = sb("relcm", [P, ET], bf16)
                base_b = sb("basem", [P, NGRP], i32)
                ext = sb("extm", [P, 1], fp32)
                m = marks_memory(spare[:, :])
                with nc.Block() as block:
                    @block.sync
                    def _(sp):
                        marks_sync(sp, m, base_b)
                        marks_sync_end(sp, m, relc[:, :], wide)

                    @block.vector
                    def _(dve):
                        step = 0 if wide else W
                        nc.vector.tensor_scalar(win[0:1, :], win[0:1, :], float(step), float(NP), ALU.add, ALU.min).then_inc(win_moved, 1)
                        nc.vector.tensor_scalar(shift[:, :], shift[:, :], -float(step), None, ALU.add).then_inc(shift_set, 1)
                        nc.vector.memset(ext[:, :], 0.0).then_inc(extent_ready, 1)
                        marks_vector(dve, m, ext, wide)
                        marks_vector_cols(dve, m, base_b, relc[:, :], relL)

        def enter():
            for eng in (nc.sync, nc.gpsimd, nc.tensor, nc.scalar, nc.vector):
                eng.nop(nofuse=True)

        def passes():
            return nc.values_load(npass[0:1, 0:1], min_val=1, max_val=NP // W + 1)

        max_edges("", False)
        more = passes()
        with nc.If(more > 1):
            enter()
            clear(mark_sems + edge_sems)
            move_windows("_w", relL, True)
            max_edges("_w", False, True)
            with nc.Fori(1, more):
                clear(mark_sems + edge_sems)
                move_windows("_a", relL)
                max_edges("_a", True)
        nc.end_ifs()
        estack.close()

        xkeep, _ = tensors(ctx)
        xa = xkeep("xa", [P, NT, D], fp32)
        with ExitStack() as ph:
            sb, ps = tensors(ph)
            u1 = sb("u1", [P, 2, D], fp32)
            u2 = sb("u2", [P, D], fp32)
            rootw = sb("rootw", [P, D], fp32)
            c1c = sb("c1c", [P, 1], fp32)
            biasc = sb("biasc", [P, 1], fp32)
            c2b = sb("c2b", [P, D], fp32)
            epsd = sb("epsd", [P, 1], fp32)
            y1 = sb("y1", [P, CW], fp32)
            hn2 = sb("hn2", [P, CH, D], fp32)
            hs2 = sb("hs2", [P, CW], fp32)
            hr2 = sb("hr2", [P, 2, CW], fp32)
            sq2 = sb("sq2", [P, CW], fp32)
            xsum2 = sb("xsum2", [P, CH], fp32)
            xvar2 = sb("xvar2", [P, CH], fp32)
            std2 = sb("std2", [P, CH], fp32)
            rs2 = sb("rs2", [P, CH], fp32)
            psA = ps("psA", [P, 1024])
            psY = ps("psY", [P, 1024])
            psX = ps("psX", [P, 1024])
            psR = ps("psR", [P, 1024])

            x_again = sem("x_again")
            wts_loaded = sem("wts_loaded")
            epsd_ready = sem("epsd_ready")
            y1_done = sem("y1_done")
            y1_relu = sem("y1_relu")
            y2_done = sem("y2_done")
            x1_added = sem("x1_added")
            x1_done = sem("x1_done")
            xsum2_done = sem("xsum2_done")
            centered2 = sem("centered2")
            squared2 = sem("squared2")
            xvar2_done = sem("xvar2_done")
            std2_done = sem("std2_done")
            rs2_done = sem("rs2_done")
            normed2 = sem("normed2")
            h2_rowed = sem("h2_rowed")
            h2_stored = [sem(f"h2_stored{n}") for n in range(2)]
            h2_transposed = sem("h2_transposed")
            h2_relu = sem("h2_relu")
            root_done = sem("root_done")
            root_kept = sem("root_kept")

            loads = [(u1[:, 0, :], U1[0:D, :]), (u1[:, 1, :], U1[D:2 * D, :]), (u2[:, :], U2), (rootw[:, :], root),
                     (c1c[:, :], col(c1)), (biasc[:, :], col(bias)), (c2b[:, :], c2.partition_broadcast(P))]

            with nc.Block() as block:
                @block.sync
                def _(sp):
                    for to, frm in loads:
                        sp.dma_start(to, frm).then_inc(wts_loaded, 16)
                    sp.dma_start(xa[:, :, :], x_rows).then_inc(x_again, 16)

                    def step(i, u):
                        k = 2 * i + u
                        sp.wait_ge(h2_rowed, k + 1)
                        sp.dma_start(h2_rows[:, bass.ds(k * CH, CH), :],
                                     hr2[:, u, :].rearrange("p (t d) -> p t d", t=CH)).then_inc(h2_stored[u], 16)
                    pairs(sp, step)
                    for u in range(2):
                        sp.wait_ge(h2_stored[u], 16 * (NCH // 2))

                @block.tensor
                def _(pe):
                    pe.wait_ge(wts_loaded, 16 * len(loads))

                    def update(k):
                        after(pe, y1_relu, k)
                        for a, n in ((0, CA), (CA, CW - CA)):
                            nc.tensor.matmul(psY[:, a:a + n], u1[:, 0, :], hT[:, bass.ds(k * CW + a, n)], start=True, stop=False)
                            ins = nc.tensor.matmul(psY[:, a:a + n], u1[:, 1, :], aggT[:, bass.ds(k * CW + a, n)], start=False, stop=True)
                        ins.then_inc(y1_done, 1)
                        pe.wait_ge(y1_relu, k + 1)
                        after(pe, x1_added, k)
                        for t in range(CH):
                            ins = nc.tensor.matmul(psX[:, t * P:(t + 1) * P], y1[:, t * P:(t + 1) * P], u2[:, :],
                                                   start=True, stop=True)
                        ins.then_inc(y2_done, 1)

                    def project(k):
                        pe.wait_ge(normed2, k + 1)
                        after(pe, h2_relu, k)
                        for t in range(CH):
                            ins = nc.tensor.transpose(psA[:, t * P:(t + 1) * P], hn2[:, t, :], ident[:, :])
                        ins.then_inc(h2_transposed, 1)
                        pe.wait_ge(h2_relu, k + 1)
                        after(pe, root_kept, k)
                        for a, n in ((0, CA), (CA, CW - CA)):
                            ins = nc.tensor.matmul(psR[:, a:a + n], rootw[:, :], hs2[:, a:a + n], start=True, stop=True)
                        ins.then_inc(root_done, 1)

                    def step(i, u):
                        k = 2 * i + u
                        update(k)
                        if there(k - 1):
                            project(k - 1)
                    pairs(pe, step)
                    project(NCH - 1)

                @block.scalar
                def _(act):
                    act.wait_ge(wts_loaded, 16 * len(loads))
                    act.wait_ge(epsd_ready, 1)

                    def update(k):
                        act.wait_ge(y1_done, k + 1)
                        after(act, y2_done, k)
                        nc.scalar.activation(y1[:, :], psY[:, 0:CW], ACT.Relu, bias=c1c[:, 0:1]).then_inc(y1_relu, 1)

                    def square(k):
                        act.wait_ge(centered2, k + 1)
                        after(act, xvar2_done, k)
                        nc.scalar.activation(sq2[:, :], flat(hn2[:, :, :]), ACT.Square).then_inc(squared2, 1)

                    def deviation(k):
                        act.wait_ge(xvar2_done, k + 1)
                        after(act, rs2_done, k)
                        nc.scalar.activation(std2[:, :], xvar2[:, :], ACT.Sqrt, bias=epsd[:, 0:1], scale=1.0 / D).then_inc(std2_done, 1)

                    def relu(k, u, n):
                        act.wait_ge(h2_transposed, k + 1)
                        after(act, root_done, k)
                        nc.scalar.activation(hs2[:, :], psA[:, 0:CW], ACT.Relu).then_inc(h2_relu, 1)
                        after(act, h2_stored[u], 16 * n)
                        nc.scalar.activation(hr2[:, u, :], flat(hn2[:, :, :]), ACT.Relu).then_inc(h2_rowed, 1)

                    def keep_root(k):
                        act.wait_ge(root_done, k + 1)
                        nc.scalar.activation(aggT[:, bass.ds(k * CW, CW)], psR[:, 0:CW], ACT.Identity,
                                             bias=biasc[:, 0:1]).then_inc(root_kept, 1)

                    def step(i, u):
                        k = 2 * i + u
                        update(k)
                        if there(k - 1):
                            relu(k - 1, 1 - u, i - 1 + u)
                        square(k)
                        if there(k - 1):
                            keep_root(k - 1)
                        deviation(k)
                    pairs(act, step)
                    relu(NCH - 1, 1, NCH // 2 - 1)
                    keep_root(NCH - 1)

                @block.vector
                def _(dve):
                    nc.vector.memset(epsd[:, :], EPS).then_inc(epsd_ready, 1)
                    nc.vector.memset(aggT[:, NP:NP + W], 0.0)
                    dve.wait_ge(wts_loaded, 16 * len(loads))
                    dve.wait_ge(x_again, 16)

                    def step(i, u):
                        k = 2 * i + u
                        xc = xa[:, bass.ds(k * CH, CH), :]
                        dve.wait_ge(y2_done, k + 1)
                        nc.vector.tensor_tensor(xc, psX[:, 0:CW].rearrange("p (t d) -> p t d", t=CH), xc, ALU.add).then_inc(x1_added, 1)
                        dve.wait_ge(x1_added, k + 1)
                        nc.vector.tensor_tensor(xc, xc, c2b[:, :].unsqueeze(1).to_broadcast([P, CH, D]), ALU.add).then_inc(x1_done, 1)
                        dve.wait_ge(x1_done, k + 1)
                        dve.nop(nofuse=True)
                        nc.vector.tensor_reduce(xsum2[:, :], xc, AX.X, ALU.add).then_inc(xsum2_done, 1)
                        dve.wait_ge(xsum2_done, k + 1)
                        after(dve, h2_transposed, k)
                        after(dve, h2_rowed, k)
                        nc.vector.scalar_tensor_tensor(out=hn2[:, :, :], in0=xsum2[:, :].unsqueeze(2).to_broadcast([P, CH, D]),
                                                       scalar=-1.0 / D, in1=xc, op0=ALU.mult, op1=ALU.add).then_inc(centered2, 1)
                        dve.wait_ge(squared2, k + 1)
                        nc.vector.tensor_reduce(xvar2[:, :], sq2[:, :].rearrange("p (t d) -> p t d", t=CH), AX.X,
                                                ALU.add).then_inc(xvar2_done, 1)
                        dve.wait_ge(std2_done, k + 1)
                        nc.vector.reciprocal(rs2[:, :], std2[:, :]).then_inc(rs2_done, 1)
                        dve.wait_ge(rs2_done, k + 1)
                        nc.vector.tensor_tensor(hn2[:, :, :], hn2[:, :, :], rs2[:, :].unsqueeze(2).to_broadcast([P, CH, D]),
                                                ALU.mult).then_inc(normed2, 1)
                    pairs(dve, step)

        l1_consts = sem("l1_consts")
        l1_iota = sem("l1_iota")
        l1_idx_ready = sem("l1_idx_ready")
        l1_gathered = [sem(f"l1_gathered{n}") for n in range(GPI)]
        types_float = sem("types_float")
        coef_step = sem("coef_step")
        hot_ready = sem("hot_ready")
        sel_ready = sem("sel_ready")
        summed = sem("summed")
        sums_copied = sem("sums_copied")
        based = sem("based")
        l1_added = sem("l1_added")
        sum_sems = [l1_consts, l1_iota, l1_idx_ready, *l1_gathered, types_float, coef_step, hot_ready, sel_ready, summed,
                    sums_copied, based, l1_added]

        def sum_edges(tag):
            with ExitStack() as ph:
                sb, ps = tensors(ph, tag)
                G = sb("G1", [P, GPI, GT, D], fp32)
                typ = sb("typ", [P, ET], i32)
                relc = sb("relc1", [P, ET], bf16)
                V = sb("V", [P, NB, D], fp32)
                compb = sb("compb", [P, NB, NR], fp32)
                rel_no = sb("rel_no", [P, NR], fp32)
                thot = sb("thot", [P, TPI, NR], fp32)
                tprod = sb("tprod", [P, TPI, NB, NR], fp32)
                coef = sb("coef", [P, 2, TPI, NB], fp32)
                hot = sb("hot", [P, 2, GT, W], fp32)
                S = sb("S", [P, 2, GT, NB, W], fp32)
                A = sb("A", [P, 2, NB, W], fp32)
                idxs = sb("idxs1", [P, GPI, GT], i32)
                psA = ps("psA1", [P, 2, 512])
                psV = ps("psV1", [P, 2, 512])

                with nc.Block() as block:
                    @block.sync
                    def _(sp):
                        sp.dma_start(V[:, :, :], basis.rearrange("b i o -> i b o")).then_inc(l1_consts, 16)
                        for b in range(NB):
                            sp.dma_start(compb[:, b, :], comp_t[b, :].partition_broadcast(P)).then_inc(l1_consts, 16)
                        sp.dma_start(relc[:, :], relc_tab).then_inc(l1_consts, 16)
                        sp.dma_start(typ[:, :], type_cols).then_inc(l1_consts, 16)

                    @block.gpsimd
                    def _(pool):
                        pool.iota(rel_no[:, :], pattern=[[1, NR]], base=0, channel_multiplier=0,
                                  allow_small_or_imprecise_dtypes=True).then_inc(l1_iota, 1)

                        def step(i, s):
                            k = GPI * i + s
                            pool.wait_ge(l1_idx_ready, k + 1)
                            pool.nop(nofuse=True)
                            if there(k - GPI):
                                pool.wait_ge(summed, k - GPI + 1)
                                pool.nop(nofuse=True)
                            for j in range(GT):
                                pool.indirect_dma_start(G[:, s, j, :], None, h2_tab,
                                                        bass.IndirectOffsetOnAxis(ap=idxs[:, s, j:j + 1], axis=0)
                                                        ).then_inc(l1_gathered[s], 16)
                        sweep(pool, step)

                    @block.tensor
                    def _(pe):
                        pe.wait_ge(l1_consts, 16 * (NB + 3))

                        def sums(i, s):
                            k, b = GPI * i + s, s % 2
                            pe.wait_ge(sel_ready, k + 1)
                            if there(k - 2):
                                pe.wait_ge(sums_copied, k - 1)
                            pe.wait_ge(l1_gathered[s], 16 * GT * (i + 1))
                            for j in range(GT):
                                ins = nc.tensor.matmul(psA[:, b, 0:NB * W], G[:, s, j, :],
                                                       S[:, b, j, :, :].rearrange("p b w -> p (b w)"),
                                                       start=j == 0, stop=j == GT - 1)
                            ins.then_inc(summed, 1)

                        def bases(k, b):
                            pe.wait_ge(sums_copied, k + 1)
                            if there(k - 2):
                                pe.wait_ge(l1_added, k - 1)
                            for n in range(NB):
                                ins = nc.tensor.matmul(psV[:, b, 0:W], V[:, n, :], A[:, b, n, :], start=n == 0, stop=n == NB - 1)
                            ins.then_inc(based, 1)

                        def step(i, s):
                            k = GPI * i + s
                            sums(i, s)
                            if there(k - 1):
                                bases(k - 1, (s + 1) % 2)
                        sweep(pe, step)
                        bases(NGRP - 1, 1)

                    @block.scalar
                    def _(act):
                        def step(i, s):
                            k, b = GPI * i + s, s % 2
                            act.wait_ge(summed, k + 1)
                            if there(k - 2):
                                act.wait_ge(based, k - 1)
                            nc.scalar.activation(A[:, b, :, :].rearrange("p b w -> p (b w)"), psA[:, b, 0:NB * W],
                                                 ACT.Copy).then_inc(sums_copied, 1)
                        sweep(act, step)

                    @block.vector
                    def _(dve):
                        dve.wait_ge(l1_consts, 16 * (NB + 3))
                        dve.wait_ge(l1_iota, 1)

                        def indices(i, s):
                            k = GPI * i + s
                            if there(k - GPI):
                                dve.wait_ge(l1_gathered[s], 16 * GT * i)
                            nc.vector.tensor_copy(idxs[:, s, :], idx0[:, bass.ds(k * GT, GT)]).then_inc(l1_idx_ready, 1)

                        def coefs(i, c):
                            dve.nop(nofuse=True)
                            nc.vector.tensor_tensor(thot[:, :, :], typ[:, bass.ds(i * TPI, TPI)].unsqueeze(2).to_broadcast([P, TPI, NR]),
                                                    rel_no[:, :].unsqueeze(1).to_broadcast([P, TPI, NR]),
                                                    ALU.is_equal).then_inc(types_float, 1)
                            dve.wait_ge(types_float, i + 1)
                            for b in range(NB):
                                ins = nc.vector.tensor_tensor(tprod[:, :, b, :], thot[:, :, :],
                                                              compb[:, b, :].unsqueeze(1).to_broadcast([P, TPI, NR]), ALU.mult)
                            ins.then_inc(coef_step, 1)
                            dve.wait_ge(coef_step, 2 * i + 1)
                            nc.vector.tensor_reduce(coef[:, c, :, :], tprod[:, :, :, :], AX.X, ALU.add).then_inc(coef_step, 1)

                        def select(i, s, c):
                            k, b = GPI * i + s, s % 2
                            nc.vector.tensor_tensor(hot[:, b, :, :], lane[:, :].unsqueeze(1).to_broadcast([P, GT, W]),
                                                    relc[:, bass.ds(k * GT, GT)].unsqueeze(2).to_broadcast([P, GT, W]),
                                                    ALU.is_equal).then_inc(hot_ready, 1)
                            dve.wait_ge(hot_ready, k + 1)
                            dve.wait_ge(coef_step, 2 * i + 2)
                            if there(k - 2):
                                dve.wait_ge(summed, k - 1)
                            for j in range(GT):
                                ins = nc.vector.tensor_tensor(S[:, b, j, :, :], hot[:, b, j, :].unsqueeze(1).to_broadcast([P, NB, W]),
                                                              coef[:, c, s * GT + j, :].unsqueeze(2).to_broadcast([P, NB, W]), ALU.mult)
                            ins.then_inc(sel_ready, 1)

                        def add(k, b):
                            dve.wait_ge(based, k + 1)
                            after(dve, l1_added, k)
                            dve.nop(nofuse=True)
                            r0 = dve.value_load(win[0:1, bass.ds(k, 1)], min_val=0, max_val=NP)
                            to = aggT[:, bass.ds(r0, W)]
                            nc.vector.tensor_tensor(to, psV[:, b, 0:W], to, ALU.add).then_inc(l1_added, 1)

                        indices(0, 0)
                        indices(0, 1)

                        def step(i, s):
                            k = GPI * i + s
                            if not (isinstance(k, int) and k + 2 >= NGRP):
                                indices(i + (s + 2) // GPI, (s + 2) % GPI)
                            if s == 0:
                                coefs(i, 0)
                            select(i, s, 0)
                            if there(k - 2):
                                add(k - 2, s % 2)
                        sweep(dve, step)
                        add(NGRP - 2, 0)
                        add(NGRP - 1, 1)

        win_reset = sem("win_reset")
        more = passes()
        with nc.If(more > 1):
            enter()
            clear(mark_sems)
            with nc.Block() as block:
                @block.sync
                def _(sp):
                    sp.dma_start(win[:, :], row(first)).then_inc(win_reset, 16)

                @block.vector
                def _(dve):
                    dve.wait_ge(win_reset, 16)
                    nc.vector.tensor_scalar(win[0:1, :], win[0:1, :], -float(W), None, ALU.add).then_inc(win_moved, 1)
                    nc.vector.memset(shift[:, :], float(W)).then_inc(win_moved, 1)
            move_windows("_b")
        nc.end_ifs()
        sum_edges("")
        more = passes()
        with nc.If(more > 1):
            enter()
            with nc.Fori(1, more):
                clear(mark_sems + sum_sems)
                move_windows("_c")
                sum_edges("_c")
        nc.end_ifs()

        with ExitStack() as ph:
            sb, ps = tensors(ph)
            ra = sb("ra", [P, 2, CW], fp32)
            psT = ps("psT", [P, 2, 1024])
            ra_done = sem("ra_done")
            ra_transposed = sem("ra_transposed")
            x2_done = sem("x2_done")
            out_stored = sem("out_stored")

            with nc.Block() as block:
                @block.scalar
                def _(act):
                    def step(i, u):
                        k = 2 * i + u
                        if there(k - 2):
                            act.wait_ge(ra_transposed, k - 1)
                        nc.scalar.activation(ra[:, u, :], aggT[:, bass.ds(k * CW, CW)], ACT.Relu).then_inc(ra_done, 1)
                    pairs(act, step)

                @block.tensor
                def _(pe):
                    def step(i, u):
                        k = 2 * i + u
                        pe.wait_ge(ra_done, k + 1)
                        if there(k - 2):
                            pe.wait_ge(x2_done, k - 1)
                        for t in range(CH):
                            ins = nc.tensor.transpose(psT[:, u, t * P:(t + 1) * P], ra[:, u, t * P:(t + 1) * P], ident[:, :])
                        ins.then_inc(ra_transposed, 1)
                    pairs(pe, step)

                @block.vector
                def _(dve):
                    def step(i, u):
                        k = 2 * i + u
                        dve.wait_ge(ra_transposed, k + 1)
                        xc = xa[:, bass.ds(k * CH, CH), :]
                        nc.vector.tensor_tensor(xc, psT[:, u, 0:CW].rearrange("p (t d) -> p t d", t=CH), xc, ALU.add).then_inc(x2_done, 1)
                    pairs(dve, step)

                @block.sync
                def _(sp):
                    def step(i, u):
                        k = 2 * i + u
                        sp.wait_ge(x2_done, k + 1)
                        sp.dma_start(out_rows[:, bass.ds(k * CH, CH), :], xa[:, bass.ds(k * CH, CH), :]).then_inc(out_stored, 16)
                    pairs(sp, step)
                    sp.wait_ge(out_stored, 16 * NCH)


_INS = ['x', 'dst', 'first', 'last', 'src_cols', 'dst_cols', 'next_cols', 'type_cols', 'w', 'W1', 'b1', 'W2', 'b2', 'U1', 'c1',
        'U2', 'c2', 'basis', 'comp_t', 'root', 'bias']


def kernel(x, src, dst, edge_type_8, edge_weight, L0_gnn_W1, L0_gnn_b1, L0_gnn_W2, L0_gnn_b2, L0_gnn_U1, L0_gnn_c1,
           L0_gnn_U2, L0_gnn_c2, L1_gnn_weight, L1_gnn_w_comp, L1_gnn_root_weight, L1_gnn_bias):
    import numpy as np
    import concourse.bacc as bacc
    from concourse.bass_utils import run_bass_kernel_spmd as run

    x, src, dst, kind, w = (np.asarray(a) for a in (x, src, dst, edge_type_8, edge_weight))
    n, d = x.shape
    e = src.shape[0]
    n_pad = -(-n // (14 * P)) * 14 * P
    e_pad = -(-e // (TPI * P)) * TPI * P
    assert n < n_pad

    def columns(v):
        return np.ascontiguousarray(v.reshape(-1, P).T)

    def padded(v, fill):
        return np.pad(v, (0, e_pad - e), constant_values=fill)

    dst_pad = padded(dst, n)
    ins = {
        'x': np.pad(x, ((0, n_pad - n), (0, 0))), 'dst': np.pad(dst_pad, (1, 0), constant_values=-1),
        'first': dst_pad[::GE], 'last': dst_pad[GE - 1::GE], 'src_cols': columns(padded(src, 0)), 'dst_cols': columns(dst_pad),
        'next_cols': columns(np.pad(dst_pad, (0, 1), constant_values=-1)[1:]), 'type_cols': columns(padded(kind, 0)),
        'w': padded(w, 0),
        'W1': L0_gnn_W1, 'b1': L0_gnn_b1, 'W2': L0_gnn_W2, 'b2': L0_gnn_b2, 'U1': L0_gnn_U1, 'c1': L0_gnn_c1,
        'U2': L0_gnn_U2, 'c2': L0_gnn_c2, 'basis': L1_gnn_weight, 'comp_t': np.asarray(L1_gnn_w_comp).T,
        'root': L1_gnn_root_weight, 'bias': L1_gnn_bias}
    nc = bacc.Bacc("TRN2", target_bir_lowering=False, num_devices=1)
    arrays, args = {}, []
    for name in _INS:
        a = np.ascontiguousarray(ins[name])
        arrays[f"in_{name}"] = a
        args.append(nc.dram_tensor(f"in_{name}", a.shape, mybir.dt.from_np(a.dtype), kind="ExternalInput").ap())
    args.append(nc.dram_tensor("out_x", (n_pad, d), mybir.dt.float32, kind="ExternalOutput").ap())
    gnn(nc, *args, n)
    r = run(nc, [arrays], core_ids=[0])
    return r.results[0]["out_x"][:n]
```

```python
import concourse.bass as bass
from concourse import mybir
from contextlib import ExitStack

P = 128
GT = 4
GE = GT * P
GPI = 8
TPI = GT * GPI
AHEAD = 5
HOT = 2
LOGW = 6
W = 1 << LOGW


def after(eng, sem, n):
    if not (isinstance(n, int) and n <= 0):
        eng.wait_ge(sem, n)


def there(k):
    return not (isinstance(k, int) and k < 0)


def gnn(nc, x, dst, first, last, src_cols, dst_cols, next_cols, type_cols, w, W1, b1, W2, b2, U1, c1, U2, c2,
        basis, comp_t, root, bias, out, n_real):
    fp32, bf16, i32 = mybir.dt.float32, mybir.dt.bfloat16, mybir.dt.int32
    ALU, ACT, AX = mybir.AluOpType, mybir.ActivationFunctionType, mybir.AxisListType
    RMAX = bass.bass_isa.ReduceOp.max

    NP, D = x.shape
    NT = NP // P
    ET = src_cols.shape[1]
    EP = ET * P
    ITERS = ET // TPI
    NGRP = ITERS * GPI
    NB, _, _ = basis.shape
    NR = comp_t.shape[1]
    CH = 7
    NCH = NT // CH
    CW = CH * P
    CA = 4 * P
    MP = 112
    MG = NGRP // MP
    HALF = 2 * GE
    EPS = 1e-5
    LOW = 3.0e38
    FAR = 2.0 ** 20
    assert NT % (2 * CH) == 0 and 7 * MG * GE // 2 <= NP and NGRP % MP == 0 and D == P and ITERS >= 3 and NCH >= 8

    p_tab = nc.dram_tensor("p_tab", (NP, D), fp32).ap()
    q_tab = nc.dram_tensor("q_tab", (NP + W, D), fp32).ap()
    h2_tab = nc.dram_tensor("h2_tab", (NP, D), fp32).ap()
    marks = nc.dram_tensor("marks", (2, EP), bf16).ap()
    relc_tab = nc.dram_tensor("relc_tab", (P, ET), bf16).ap()

    p_rows = p_tab.rearrange("(t p) d -> p t d", p=P)
    q_rows = q_tab[0:NP, :].rearrange("(t p) d -> p t d", p=P)
    h2_rows = h2_tab.rearrange("(t p) d -> p t d", p=P)
    x_rows = x.rearrange("(t p) d -> p t d", p=P)
    out_rows = out.rearrange("(t p) d -> p t d", p=P)

    ctx = ExitStack()

    def sem(name):
        return ctx.enter_context(nc.semaphore(name))

    def tensors(stack, tag=""):
        def sb(name, shape, dt):
            return stack.enter_context(nc.sbuf_tensor(name + tag, shape, dt))

        def ps(name, shape):
            return stack.enter_context(nc.psum_tensor(name + tag, shape, fp32))
        return sb, ps

    def row(v):
        return v.rearrange("(a n) -> a n", a=1)

    def col(v):
        return v.rearrange("(n a) -> n a", a=1)

    def flat(v):
        return v.rearrange("p a d -> p (a d)")

    def pairs(eng, step, lead=1):
        for i in range(lead):
            for u in range(2):
                step(i, u)
        with eng.Fori(lead, NCH // 2 - 1) as i:
            for u in range(2):
                step(i, u)
        for u in range(2):
            step(NCH // 2 - 1, u)

    def sweep(eng, step):
        for s in range(GPI):
            step(0, s)
        with eng.Fori(1, ITERS - 1) as i:
            for s in range(GPI):
                step(i, s)
        for s in range(GPI):
            step(ITERS - 1, s)

    def marks_memory(work):
        n = MG * GE
        dI, pI = work[:, 0:n].bitcast(i32), work[:, n:2 * n].bitcast(i32)
        b16 = work[:, 2 * n:2 * n + 3 * n // 2].bitcast(bf16)
        return dI, pI, b16[:, 0:n], b16[:, n:2 * n], b16[:, 2 * n:3 * n]

    def marks_sync(sp, m, base_b):
        dI, pI, cont, lowm, relb = m
        sp.dma_start(dI[0:MP, :], dst[1:EP + 1].rearrange("(p e) -> p e", p=MP)).then_inc(dst_loaded, 16)
        sp.dma_start(pI[0:MP, :], dst[0:EP].rearrange("(p e) -> p e", p=MP)).then_inc(prev_loaded, 16)
        sp.dma_start(base_b[:, :], first.partition_broadcast(P)).then_inc(base_loaded, 16)

    def marks_sync_store(sp, m, wide=False):
        dI, pI, cont, lowm, relb = m
        sp.wait_ge(mark_step, 4 if wide else 3)
        sp.dma_start(marks[0, :].rearrange("(p e) -> p e", p=MP), relb[0:MP, :]).then_inc(marks_stored, 16)
        sp.dma_start(marks[1, :].rearrange("(p e) -> p e", p=MP), lowm[0:MP, :]).then_inc(marks_stored, 16)
        sp.wait_ge(extent_ready, 2)
        sp.dma_start(dI[:, 0:ET], dst_cols).then_inc(cols_loaded, 16)
        sp.dma_start(pI[:, 0:ET], next_cols).then_inc(next_loaded, 16)

    def marks_sync_end(sp, relc):
        sp.wait_ge(cols_step, 2)
        sp.dma_start(relc_tab, relc).then_inc(relc_stored, 16)
        sp.wait_ge(marks_stored, 32)
        sp.wait_ge(relc_stored, 16)

    def marks_vector(dve, m, ext, wide=False):
        dI, pI, cont, lowm, relb = (v[0:MP, :] for v in m)
        g3 = lambda v: v.rearrange("p (g e) -> p g e", e=GE)
        base = g3(dI)[:, :, 0:1].to_broadcast([MP, MG, GE])
        dve.wait_ge(dst_loaded, 16)
        dve.wait_ge(prev_loaded, 16)
        nc.vector.tensor_tensor(cont, dI, pI, ALU.is_equal).then_inc(mark_step, 1)
        dve.wait_ge(mark_step, 1)
        nc.vector.tensor_scalar(lowm, cont, -1.0, LOW, ALU.add, ALU.mult).then_inc(mark_step, 1)
        dve.wait_ge(shift_set, 1)
        nc.vector.scalar_tensor_tensor(out=g3(relb), in0=g3(dI), scalar=shift[0:MP, 0:1], in1=base,
                                       op0=ALU.add, op1=ALU.subtract).then_inc(mark_step, 1)
        if wide:
            dve.wait_ge(mark_step, 2)
            last = g3(dI)[:, :, GE - 1:GE].to_broadcast([MP, MG, GE])
            nc.vector.tensor_tensor(g3(cont), g3(dI), last, ALU.not_equal).then_inc(wide_step, 1)
            dve.wait_ge(wide_step, 1)
            nc.vector.tensor_scalar(cont, cont, FAR, W - 0.5, ALU.mult, ALU.add).then_inc(wide_step, 1)
            dve.wait_ge(wide_step, 2)
            dve.wait_ge(mark_step, 3)
            nc.vector.tensor_tensor(relb, relb, cont, ALU.min).then_inc(mark_step, 1)
        span = pI.bitcast(fp32)
        dve.wait_ge(mark_step, 2)
        nc.vector.tensor_tensor(g3(span), g3(dI), base, ALU.subtract).then_inc(span_step, 1)
        dve.wait_ge(span_step, 1)
        nc.vector.scalar_tensor_tensor(out=span, in0=dI, scalar=float(n_real), in1=span,
                                       op0=ALU.is_lt, op1=ALU.mult).then_inc(span_step, 1)
        dve.wait_ge(span_step, 2)
        dve.wait_ge(extent_ready, 1)
        nc.vector.tensor_reduce(ext[0:MP, 0:1], span, AX.X, ALU.max).then_inc(extent_ready, 1)

    def marks_vector_places(dve, m, base_b, relc):
        dcol, ncol = m[0][:, 0:ET], m[1][:, 0:ET]
        islast = m[2][:, 0:ET]
        g3 = lambda v: v.rearrange("p (g t) -> p g t", t=GT)
        dve.wait_ge(cols_loaded, 16)
        dve.wait_ge(next_loaded, 16)
        dve.wait_ge(base_loaded, 16)
        nc.vector.tensor_tensor(islast, dcol, ncol, ALU.not_equal).then_inc(cols_step, 1)
        nc.vector.scalar_tensor_tensor(out=g3(relc), in0=g3(dcol), scalar=shift[:, 0:1],
                                       in1=base_b[:, :].unsqueeze(2).to_broadcast([P, NGRP, GT]),
                                       op0=ALU.add, op1=ALU.subtract).then_inc(cols_step, 1)

    def marks_vector_lasts(dve, m, relc, relL):
        dve.wait_ge(cols_step, 2)
        nc.vector.scalar_tensor_tensor(out=relL[:, :], in0=relc, scalar=1.0, in1=m[2][:, 0:ET],
                                       op0=ALU.add, op1=ALU.mult).then_inc(cols_step, 1)
        dve.wait_ge(cols_step, 3)
        nc.vector.tensor_scalar(relL[:, :], relL[:, :], -1.0, None, ALU.add).then_inc(cols_step, 1)
        dve.wait_ge(cols_step, 4)

    with ctx:
        keep, _ = tensors(ctx)
        aggT = keep("aggT", [P, NP + W], fp32)
        ident = keep("ident", [P, P], fp32)
        idx0 = keep("idx0", [P, ET], i32)
        win = keep("win", [1, NGRP], i32)
        lane = keep("lane", [P, W], fp32)
        pidx = keep("pidx", [P, 1], fp32)
        shift = keep("shift", [P, 1], fp32)
        npass = keep("npass", [1, 1], i32)
        work = aggT

        dst_loaded = sem("dst_loaded")
        prev_loaded = sem("prev_loaded")
        base_loaded = sem("base_loaded")
        cols_loaded = sem("cols_loaded")
        next_loaded = sem("next_loaded")
        mark_step = sem("mark_step")
        span_step = sem("span_step")
        cols_step = sem("cols_step")
        extent_ready = sem("extent_ready")
        marks_stored = sem("marks_stored")
        relc_stored = sem("relc_stored")
        shift_set = sem("shift_set")
        wide_step = sem("wide_step")
        mark_sems = [dst_loaded, prev_loaded, base_loaded, cols_loaded, next_loaded, mark_step, span_step, cols_step,
                     extent_ready, marks_stored, relc_stored, shift_set, wide_step]

        hT = keep("hT", [P, NT * P], fp32)
        estack = ctx.enter_context(ExitStack())
        ekeep, _ = tensors(estack)
        relL = ekeep("relL", [P, ET], bf16)
        with ExitStack() as ph:
            sb, ps = tensors(ph)
            xa = sb("xa0", [P, NT, D], fp32)
            w1ab = sb("w1ab", [P, 2, D], fp32)
            xsum = sb("xsum", [P, 2, CH], fp32)
            xvar = sb("xvar", [P, 2, CH], fp32)
            std = sb("std", [P, 2, CH], fp32)
            rstd = sb("rstd", [P, 2, CH], fp32)
            epsc = sb("epsc", [P, 1], fp32)
            hn = sb("hn", [P, 2, CH, D], fp32)
            hs = sb("hs", [P, CW], fp32)
            pq = sb("pq", [P, 2, CH, 2, D], fp32)
            relc = sb("relc", [P, ET], bf16)
            base_b = sb("base_b", [P, NGRP], i32)
            ext = sb("ext", [P, 1], fp32)
            exta = sb("exta", [P, 1], fp32)
            extI = sb("extI", [P, 2], i32)
            zrow = sb("zrow", [W, D], fp32)
            m = marks_memory(work[:, :])
            psH = ps("psH", [P, 1024])
            psQ = ps("psQ", [P, 2048])
            psS = ps("psS", [P, 1024])

            x_loaded = sem("x_loaded")
            w1_loaded = sem("w1_loaded")
            idx_loaded = sem("idx_loaded")
            pad_zeroed = sem("pad_zeroed")
            ident_zeroed = sem("ident_zeroed")
            ident_ready = sem("ident_ready")
            eps_ready = sem("eps_ready")
            xsum_done = sem("xsum_done")
            centered = sem("centered")
            squared = sem("squared")
            xvar_done = sem("xvar_done")
            std_done = sem("std_done")
            rstd_done = sem("rstd_done")
            normed = sem("normed")
            h_transposed = sem("h_transposed")
            h_relu = sem("h_relu")
            h_kept = sem("h_kept")
            pq_done = sem("pq_done")
            pq_copied_a = sem("pq_copied_a")
            pq_copied_b = sem("pq_copied_b")
            p_stored = [sem(f"p_stored{n}") for n in range(2)]
            q_stored = [sem(f"q_stored{n}") for n in range(2)]
            extent_joined = sem("extent_joined")
            pass_step = sem("pass_step")
            pad_stored = sem("pad_stored")
            win_loaded = sem("win_loaded")

            with nc.Block() as block:
                @block.sync
                def _(sp):
                    marks_sync(sp, m, base_b)
                    sp.dma_start(xa[:, :, :], x_rows).then_inc(x_loaded, 16)
                    sp.dma_start(w1ab[:, :, :], W1[0:2 * D, :].rearrange("(a p) d -> p a d", a=2)).then_inc(w1_loaded, 16)
                    sp.dma_start(idx0[:, :], src_cols).then_inc(idx_loaded, 16)
                    sp.dma_start(win[:, :], row(first)).then_inc(win_loaded, 16)
                    marks_sync_store(sp, m)

                    def step(i, u):
                        k = 2 * i + u
                        sp.wait_ge(pq_copied_a, k + 1)
                        sp.wait_ge(pq_copied_b, k + 1)
                        sp.dma_start(p_rows[:, bass.ds(k * CH, CH), :], pq[:, u, :, 0, :]).then_inc(p_stored[u], 16)
                        sp.dma_start(q_rows[:, bass.ds(k * CH, CH), :], pq[:, u, :, 1, :]).then_inc(q_stored[u], 16)
                    pairs(sp, step)
                    sp.wait_ge(pad_zeroed, 1)
                    sp.dma_start(q_tab[NP:NP + W, :], zrow[:, :]).then_inc(pad_stored, 16)
                    marks_sync_end(sp, relc[:, :])
                    for u in range(2):
                        sp.wait_ge(p_stored[u], 16 * (NCH // 2))
                        sp.wait_ge(q_stored[u], 16 * (NCH // 2))
                    sp.wait_ge(pad_stored, 16)
                    sp.wait_ge(idx_loaded, 16)
                    sp.wait_ge(win_loaded, 16)

                @block.gpsimd
                def _(pool):
                    pool.memset(ident[:, :], 0.0).then_inc(ident_zeroed, 1)
                    pool.wait_ge(ident_zeroed, 1)
                    pool.affine_select(out=ident[:, :], in_=ident[:, :], compare_op=ALU.not_equal, fill=1.0,
                                       base=0, pattern=[[-1, P]], channel_multiplier=1).then_inc(ident_ready, 1)
                    pool.iota(lane[:, :], pattern=[[1, W]], base=0, channel_multiplier=0,
                              allow_small_or_imprecise_dtypes=True)
                    pool.iota(pidx[:, :], pattern=[[0, 1]], base=0, channel_multiplier=1,
                              allow_small_or_imprecise_dtypes=True)
                    pool.memset(shift[:, :], 0.0).then_inc(shift_set, 1)
                    pool.memset(zrow[:, :], 0.0).then_inc(pad_zeroed, 1)
                    pool.wait_ge(extent_ready, 2)
                    pool.partition_all_reduce(exta[:, :], ext[:, :], P, RMAX).then_inc(extent_joined, 1)

                @block.scalar
                def _(act):
                    act.wait_ge(eps_ready, 1)

                    def square(k, u):
                        act.wait_ge(centered, k + 1)
                        after(act, xvar_done, k)
                        nc.scalar.activation(psS[:, 0:CW], hn[:, u, :, :].rearrange("p t d -> p (t d)"), ACT.Square).then_inc(squared, 1)

                    def deviation(k, u):
                        act.wait_ge(xvar_done, k + 1)
                        nc.scalar.activation(std[:, u, :], xvar[:, u, :], ACT.Sqrt, bias=epsc[:, 0:1], scale=1.0 / D).then_inc(std_done, 1)

                    def relu(k):
                        act.wait_ge(h_transposed, k + 1)
                        after(act, pq_done, k)
                        nc.scalar.activation(hs[:, :], psH[:, 0:CW], ACT.Relu).then_inc(h_relu, 1)
                        nc.scalar.activation(hT[:, bass.ds(k * CW, CW)], psH[:, 0:CW], ACT.Relu).then_inc(h_kept, 1)

                    def copy_pq(k, u, n):
                        act.wait_ge(pq_done, k + 1)
                        after(act, p_stored[u], n * 16)
                        after(act, q_stored[u], n * 16)
                        nc.scalar.activation(pq[:, u, 0:4, :, :].rearrange("p t a d -> p (t a d)"), psQ[:, 0:1024],
                                             ACT.Copy).then_inc(pq_copied_a, 1)
                    square(0, 0)

                    def step(i, u):
                        k = 2 * i + u
                        deviation(k, u)
                        if not (isinstance(k, int) and k + 1 >= NCH):
                            square(k + 1, 1 - u)
                        if there(k - 1):
                            copy_pq(k - 1, 1 - u, i - 1 + u)
                        relu(k)
                    pairs(act, step)
                    copy_pq(NCH - 1, 1, NCH // 2 - 1)

                @block.tensor
                def _(pe):
                    pe.wait_ge(ident_ready, 1)
                    pe.wait_ge(w1_loaded, 16)

                    def step(i, u):
                        k = 2 * i + u
                        pe.wait_ge(normed, k + 1)
                        after(pe, h_kept, k)
                        for t in range(CH):
                            ins = nc.tensor.transpose(psH[:, t * P:(t + 1) * P], hn[:, u, t, :], ident[:, :])
                        ins.then_inc(h_transposed, 1)
                        pe.wait_ge(h_relu, k + 1)
                        after(pe, pq_copied_a, k)
                        after(pe, pq_copied_b, k)
                        for t in range(CH):
                            ins = nc.tensor.matmul(psQ[:, t * 2 * D:(t + 1) * 2 * D], hs[:, t * P:(t + 1) * P],
                                                   w1ab[:, :, :].rearrange("p a d -> p (a d)"), start=True, stop=True)
                        ins.then_inc(pq_done, 1)
                    pairs(pe, step)

                @block.vector
                def _(dve):
                    nc.vector.memset(epsc[:, :], EPS).then_inc(eps_ready, 1)
                    nc.vector.memset(ext[:, :], 0.0).then_inc(extent_ready, 1)
                    marks_vector(dve, m, ext)
                    dve.wait_ge(x_loaded, 16)

                    def center(k, u):
                        xc = xa[:, bass.ds(k * CH, CH), :]
                        nc.vector.tensor_reduce(xsum[:, u, :], xc, AX.X, ALU.add).then_inc(xsum_done, 1)
                        dve.wait_ge(xsum_done, k + 1)
                        if there(k - 2):
                            dve.wait_ge(h_transposed, k - 1)
                        nc.vector.scalar_tensor_tensor(out=hn[:, u, :, :], in0=xsum[:, u, :].unsqueeze(2).to_broadcast([P, CH, D]),
                                                       scalar=-1.0 / D, in1=xc, op0=ALU.mult, op1=ALU.add).then_inc(centered, 1)

                    def scale(k, u):
                        dve.wait_ge(std_done, k + 1)
                        nc.vector.reciprocal(rstd[:, u, :], std[:, u, :]).then_inc(rstd_done, 1)
                        dve.wait_ge(rstd_done, k + 1)
                        nc.vector.tensor_tensor(hn[:, u, :, :], hn[:, u, :, :], rstd[:, u, :].unsqueeze(2).to_broadcast([P, CH, D]),
                                                ALU.mult).then_inc(normed, 1)

                    def variance(k, u):
                        dve.wait_ge(squared, k + 1)
                        nc.vector.tensor_reduce(xvar[:, u, :], psS[:, 0:CW].rearrange("p (t d) -> p t d", t=CH), AX.X,
                                                ALU.add).then_inc(xvar_done, 1)

                    def copy_pq(k, u, n):
                        dve.wait_ge(pq_done, k + 1)
                        after(dve, p_stored[u], n * 16)
                        after(dve, q_stored[u], n * 16)
                        nc.vector.tensor_copy(pq[:, u, 4:CH, :, :].rearrange("p t a d -> p (t a d)"),
                                              psQ[:, 1024:CH * 2 * D]).then_inc(pq_copied_b, 1)
                    center(0, 0)

                    def step(i, u):
                        k = 2 * i + u
                        variance(k, u)
                        if not (isinstance(k, int) and k + 1 >= NCH):
                            dve.nop(nofuse=True)
                            center(k + 1, 1 - u)
                        scale(k, u)
                        if there(k - 1):
                            copy_pq(k - 1, 1 - u, i - 1 + u)
                        if isinstance(k, int) and k == 1:
                            marks_vector_places(dve, m, base_b, relc[:, :])
                        if isinstance(k, int) and k == NCH - 2:
                            marks_vector_lasts(dve, m, relc[:, :], relL)
                    pairs(dve, step)
                    copy_pq(NCH - 1, 1, NCH // 2 - 1)

                    dve.wait_ge(extent_joined, 1)
                    nc.vector.tensor_copy(extI[:, 0:1], exta[:, :]).then_inc(pass_step, 1)
                    dve.wait_ge(pass_step, 1)
                    nc.vector.tensor_scalar(extI[:, 1:2], extI[:, 0:1], LOGW, None, ALU.logical_shift_right).then_inc(pass_step, 1)
                    dve.wait_ge(pass_step, 2)
                    nc.vector.tensor_scalar(npass[0:1, 0:1], extI[0:1, 1:2], 1.0, None, ALU.add).then_inc(pass_step, 1)
                    dve.wait_ge(pass_step, 3)

        consts_loaded = sem("consts_loaded")
        w1c_loaded = sem("w1c_loaded")
        agg_zeroed = sem("agg_zeroed")
        idx_ready = sem("idx_ready")
        gathered = [sem(f"gathered{n}") for n in range(GPI)]
        qwin_loaded = [sem(f"qwin_loaded{n}") for n in range(GPI)]
        places_loaded = [sem(f"places_loaded{n}") for n in range(GPI // 2)]
        masks_loaded = [sem(f"masks_loaded{n}") for n in range(GPI // 2)]
        wgt_loaded = [sem(f"wgt_loaded{n}") for n in range(GPI // 2)]
        onehot_ready = sem("onehot_ready")
        z_done = sem("z_done")
        relu_done = sem("relu_done")
        msg_done = sem("msg_done")
        scanned = sem("scanned")
        back_done = sem("back_done")
        picks_ready = sem("picks_ready")
        picked = sem("picked")
        added = sem("added")
        tail_loaded = sem("tail_loaded")
        place_ready = sem("place_ready")
        edge_sems = [tail_loaded, place_ready, consts_loaded, w1c_loaded, agg_zeroed, idx_ready, *gathered, *qwin_loaded, *places_loaded,
                     *masks_loaded, *wgt_loaded, onehot_ready, z_done, relu_done, msg_done, scanned, back_done,
                     picks_ready, picked, added]

        def clear(sems):
            with nc.Block() as block:
                @block.gpsimd
                def _(pool):
                    pool.dma_reset()
                    for s in sems:
                        pool.sem_clear(s)

        def max_edges(tag, again, wide=False):
            WQ = W + wide
            with ExitStack() as ph:
                sb, ps = tensors(ph, tag)
                G = sb("G", [P, GPI, GT, D], fp32)
                Qw = sb("Qw", [WQ + 1, GPI, D], fp32)
                oh = sb("oh", [WQ + 1, GPI, GE], fp32)
                Z = sb("Z", [P, 2, GE], fp32)
                R = sb("R", [P, 2, GE], fp32)
                O = sb("O", [P, 2, GE], fp32)
                E = sb("E", [P, 2, GT, W], fp32)
                pl = sb("pl", [WQ, GPI // 2, HALF], bf16)
                mk = sb("mk", [P, GPI // 2, HALF], bf16)
                idxs = sb("idxs", [P, GPI, GT], i32)
                w2 = sb("w2", [P, D], fp32)
                b1c = sb("b1c", [P, 1], fp32)
                b2b = sb("b2b", [P, D], fp32)
                place = sb("place", [P, 1], fp32)
                if wide:
                    tail = sb("tail", [1, NGRP], i32)
                psZ = ps("psZ", [P, 2, GE])
                psM = ps("psM", [P, 2, GE])
                psB = ps("psB", [P, 2, GE])
                psE = ps("psE", [P, 2, GE])

                with nc.Block() as block:
                    @block.sync
                    def _(sp):
                        for s in range(GPI):
                            sp.dma_start(Qw[WQ:WQ + 1, s, :], W1[2 * D:2 * D + 1, :]).then_inc(w1c_loaded, 16)
                        sp.dma_start(w2[:, :], W2).then_inc(consts_loaded, 16)
                        sp.dma_start(b1c[:, :], col(b1)).then_inc(consts_loaded, 16)
                        sp.dma_start(b2b[:, :], b2.partition_broadcast(P)).then_inc(consts_loaded, 16)

                        if wide:
                            sp.dma_start(tail[:, :], row(last)).then_inc(tail_loaded, 16)
                            sp.wait_ge(tail_loaded, 16)

                        def step(i, s):
                            k = GPI * i + s
                            if there(k - GPI):
                                sp.wait_ge(z_done, k - GPI + 1 + (s % 2 == 0))
                            sp.nop(nofuse=True)
                            r0 = sp.value_load(win[0:1, bass.ds(k, 1)], min_val=0, max_val=NP)
                            sp.dma_start(Qw[0:W, s, :], q_tab[bass.ds(r0, W), :]).then_inc(qwin_loaded[s], 16)
                            if wide:
                                r1 = sp.value_load(tail[0:1, bass.ds(k, 1)], min_val=0, max_val=NP)
                                sp.dma_start(Qw[W:WQ, s, :], q_tab[bass.ds(r1, 1), :]).then_inc(qwin_loaded[s], 16)
                            if s % 2 == 0:
                                h = s // 2
                                sp.dma_start(oh[WQ:WQ + 1, s:s + 2, :].rearrange("p a e -> p (a e)"),
                                             row(w)[:, bass.ds(k * GE, HALF)]).then_inc(wgt_loaded[h], 16)
                                if there(k - GPI):
                                    sp.wait_ge(scanned, k - GPI + 3)
                                    sp.nop(nofuse=True)
                                sp.dma_start(pl[:, h, :], marks[0, bass.ds(k * GE, HALF)].partition_broadcast(WQ)
                                             ).then_inc(places_loaded[h], 16)
                                sp.dma_start(mk[:, h, :], marks[1, bass.ds(k * GE, HALF)].partition_broadcast(P)
                                             ).then_inc(masks_loaded[h], 16)
                        sweep(sp, step)

                    @block.gpsimd
                    def _(pool):
                        def step(i, s):
                            k = GPI * i + s
                            pool.wait_ge(idx_ready, k + 1)
                            pool.nop(nofuse=True)
                            if there(k - GPI):
                                pool.wait_ge(z_done, k - GPI + 1)
                                pool.nop(nofuse=True)
                            for j in range(GT):
                                pool.indirect_dma_start(G[:, s, j, :], None, p_tab,
                                                        bass.IndirectOffsetOnAxis(ap=idxs[:, s, j:j + 1], axis=0)
                                                        ).then_inc(gathered[s], 16)
                        sweep(pool, step)

                    @block.tensor
                    def _(pe):
                        pe.wait_ge(consts_loaded, 48)
                        pe.wait_ge(w1c_loaded, 16 * GPI)

                        def z(i, s):
                            k, b = GPI * i + s, s % 2
                            if there(k - 2):
                                pe.wait_ge(relu_done, k - 1)
                            pe.wait_ge(gathered[s], 16 * GT * (i + 1))
                            for j in range(GT):
                                nc.tensor.matmul(psZ[:, b, j * P:(j + 1) * P], G[:, s, j, :], ident[:, :], is_transpose=True,
                                                 start=j == 0, stop=False)
                            pe.wait_ge(onehot_ready, k + 1)
                            pe.wait_ge(wgt_loaded[s // 2], 16 * (i + 1))
                            pe.wait_ge(qwin_loaded[s], (16 + 16 * wide) * (i + 1))
                            nc.tensor.matmul(psZ[:, b, :], Qw[:, s, :], oh[:, s, :], start=False, stop=True).then_inc(z_done, 1)

                        def msg(k, b):
                            pe.wait_ge(relu_done, k + 1)
                            if there(k - 2):
                                pe.wait_ge(scanned, k)
                            nc.tensor.matmul(psM[:, b, :], w2[:, :], Z[:, b, :], start=True, stop=True).then_inc(msg_done, 1)

                        def back(k, b):
                            pe.wait_ge(scanned, k + 2)
                            if there(k - 2):
                                pe.wait_ge(picks_ready, k - 1)
                            for j in range(GT):
                                ins = nc.tensor.transpose(psB[:, b, j * P:(j + 1) * P], R[:, b, j * P:(j + 1) * P], ident[:, :])
                            ins.then_inc(back_done, 1)

                        def pick(k, b):
                            pe.wait_ge(picks_ready, k + 1)
                            if there(k - 2):
                                pe.wait_ge(added, k - 1)
                            for j in range(GT):
                                ins = nc.tensor.matmul(psE[:, b, 0:W], O[:, b, j * P:(j + 1) * P], E[:, b, j, :],
                                                       start=j == 0, stop=j == GT - 1)
                            ins.then_inc(picked, 1)

                        def step(i, s):
                            k = GPI * i + s
                            z(i, s)
                            if there(k - 1):
                                msg(k - 1, (s + 1) % 2)
                            if there(k - 2):
                                back(k - 2, s % 2)
                            if there(k - 3):
                                pick(k - 3, (s + 1) % 2)
                        sweep(pe, step)
                        msg(NGRP - 1, 1)
                        back(NGRP - 2, 0)
                        pick(NGRP - 3, 1)
                        back(NGRP - 1, 1)
                        pick(NGRP - 2, 0)
                        pick(NGRP - 1, 1)

                    @block.scalar
                    def _(act):
                        act.wait_ge(consts_loaded, 48)

                        def step(i, s):
                            k, b = GPI * i + s, s % 2
                            act.wait_ge(z_done, k + 1)
                            if there(k - 2):
                                act.wait_ge(msg_done, k - 1)
                            nc.scalar.activation(Z[:, b, :], psZ[:, b, :], ACT.Relu, bias=b1c[:, 0:1]).then_inc(relu_done, 1)
                        sweep(act, step)

                    @block.vector
                    def _(dve):
                        nc.vector.tensor_scalar(place[:, :], pidx[:, :], W - 0.5, None, ALU.min).then_inc(place_ready, 1)
                        nc.vector.memset(R[:, 1, :], 0.0).then_inc(scanned, 1)

                        def indices(i, s):
                            k = GPI * i + s
                            if there(k - GPI):
                                dve.wait_ge(gathered[s], 16 * GT * i)
                            nc.vector.tensor_copy(idxs[:, s, :], idx0[:, bass.ds(k * GT, GT)]).then_inc(idx_ready, 1)

                        def onehot(i, s):
                            k, b = GPI * i + s, s % 2
                            if there(k - GPI):
                                dve.wait_ge(z_done, k - GPI + 1)
                            dve.wait_ge(places_loaded[s // 2], 16 * (i + 1))
                            nc.vector.tensor_scalar(oh[0:WQ, s, :], pl[:, s // 2, b * GE:(b + 1) * GE], place[0:WQ, 0:1], None,
                                                    ALU.is_equal).then_inc(onehot_ready, 1)

                        def scan(i, s):
                            k, b = GPI * i + s, s % 2
                            dve.wait_ge(masks_loaded[s // 2], 16 * (i + 1))
                            dve.wait_ge(msg_done, k + 1)
                            dve.wait_ge(scanned, k + 1)
                            if there(k - 2):
                                dve.wait_ge(back_done, k - 1)
                            nc.vector.tensor_tensor_scan(R[:, b, :], mk[:, s // 2, b * GE:(b + 1) * GE], psM[:, b, :],
                                                         R[:, 1 - b, GE - 1:GE], ALU.add, ALU.max).then_inc(scanned, 1)

                        def picks(k, b):
                            dve.wait_ge(back_done, k + 1)
                            if there(k - 2):
                                dve.wait_ge(picked, k - 1)
                            nc.vector.tensor_tensor(O[:, b, :].rearrange("p (j d) -> p j d", j=GT),
                                                    psB[:, b, :].rearrange("p (j d) -> p j d", j=GT),
                                                    b2b[:, :].unsqueeze(1).to_broadcast([P, GT, D]), ALU.add)
                            nc.vector.tensor_tensor(E[:, b, :, :], lane[:, :].unsqueeze(1).to_broadcast([P, GT, W]),
                                                    relL[:, bass.ds(k * GT, GT)].unsqueeze(2).to_broadcast([P, GT, W]),
                                                    ALU.is_equal).then_inc(picks_ready, 1)

                        def add(k, b):
                            dve.wait_ge(picked, k + 1)
                            after(dve, added, k)
                            dve.nop(nofuse=True)
                            r0 = dve.value_load(win[0:1, bass.ds(k, 1)], min_val=0, max_val=NP)
                            to = aggT[:, bass.ds(r0, W)]
                            nc.vector.tensor_tensor(to, psE[:, b, 0:W], to, ALU.add).then_inc(added, 1)

                        for s in range(AHEAD):
                            indices(0, s)
                        if not again:
                            nc.vector.memset(aggT[:, 0:NP + W], 0.0).then_inc(agg_zeroed, 1)
                        dve.wait_ge(place_ready, 1)
                        for s in range(HOT):
                            onehot(0, s)
                        dve.wait_ge(consts_loaded, 48)
                        if not again:
                            dve.wait_ge(agg_zeroed, 1)

                        def step(i, s):
                            k = GPI * i + s
                            if not (isinstance(k, int) and k + HOT >= NGRP):
                                onehot(i + (s + HOT) // GPI, (s + HOT) % GPI)
                            if not (isinstance(k, int) and k + AHEAD >= NGRP):
                                indices(i + (s + AHEAD) // GPI, (s + AHEAD) % GPI)
                            if there(k - 1):
                                scan(i - (s == 0), (s + GPI - 1) % GPI)
                            if there(k - 2):
                                picks(k - 2, s % 2)
                            if there(k - 3):
                                add(k - 3, (s + 1) % 2)
                        sweep(dve, step)
                        scan(ITERS - 1, GPI - 1)
                        picks(NGRP - 2, 0)
                        add(NGRP - 3, 1)
                        picks(NGRP - 1, 1)
                        add(NGRP - 2, 0)
                        add(NGRP - 1, 1)

        win_moved = sem("win_moved")

        def move_windows(tag, relL=None, wide=False):
            with ExitStack() as ph:
                sb, _ = tensors(ph, tag)
                if relL is None:
                    spare = hT
                    relL = sb("relLm", [P, ET], bf16)
                else:
                    spare = sb("spare", [P, 7 * MG * GE // 2], fp32)
                relc = sb("relcm", [P, ET], bf16)
                base_b = sb("basem", [P, NGRP], i32)
                ext = sb("extm", [P, 1], fp32)
                m = marks_memory(spare[:, :])
                with nc.Block() as block:
                    @block.sync
                    def _(sp):
                        marks_sync(sp, m, base_b)
                        marks_sync_store(sp, m, wide)
                        marks_sync_end(sp, relc[:, :])

                    @block.vector
                    def _(dve):
                        step = 0 if wide else W
                        nc.vector.tensor_scalar(win[0:1, :], win[0:1, :], float(step), float(NP), ALU.add, ALU.min).then_inc(win_moved, 1)
                        nc.vector.tensor_scalar(shift[:, :], shift[:, :], -float(step), None, ALU.add).then_inc(shift_set, 1)
                        nc.vector.memset(ext[:, :], 0.0).then_inc(extent_ready, 1)
                        marks_vector(dve, m, ext, wide)
                        marks_vector_places(dve, m, base_b, relc[:, :])
                        marks_vector_lasts(dve, m, relc[:, :], relL)

        def enter():
            for eng in (nc.sync, nc.gpsimd, nc.tensor, nc.scalar, nc.vector):
                eng.nop(nofuse=True)

        def passes():
            return nc.values_load(npass[0:1, 0:1], min_val=1, max_val=NP // W + 1)

        max_edges("", False)
        more = passes()
        with nc.If(more > 1):
            enter()
            clear(mark_sems + edge_sems)
            move_windows("_w", relL, True)
            max_edges("_w", False, True)
            with nc.Fori(1, more):
                clear(mark_sems + edge_sems)
                move_windows("_a", relL)
                max_edges("_a", True)
        nc.end_ifs()
        estack.close()

        xkeep, _ = tensors(ctx)
        xa = xkeep("xa", [P, NT, D], fp32)
        with ExitStack() as ph:
            sb, ps = tensors(ph)
            u1 = sb("u1", [P, 2, D], fp32)
            u2 = sb("u2", [P, D], fp32)
            rootw = sb("rootw", [P, D], fp32)
            c1c = sb("c1c", [P, 1], fp32)
            biasc = sb("biasc", [P, 1], fp32)
            c2b = sb("c2b", [P, D], fp32)
            epsd = sb("epsd", [P, 1], fp32)
            y1 = sb("y1", [P, CW], fp32)
            hn2 = sb("hn2", [P, 2, CH, D], fp32)
            hs2 = sb("hs2", [P, CW], fp32)
            hr2 = sb("hr2", [P, 2, CW], fp32)
            sq2 = sb("sq2", [P, CW], fp32)
            xsum2 = sb("xsum2", [P, CH], fp32)
            xvar2 = sb("xvar2", [P, CH], fp32)
            std2 = sb("std2", [P, CH], fp32)
            rs2 = sb("rs2", [P, CH], fp32)
            psA = ps("psA", [P, 1024])
            psY = ps("psY", [P, 1024])
            psX = ps("psX", [P, 1024])
            psR = ps("psR", [P, 1024])

            x_first = sem("x_first")
            x_again = sem("x_again")
            wts_loaded = sem("wts_loaded")
            epsd_ready = sem("epsd_ready")
            y1_done = sem("y1_done")
            y1_relu = sem("y1_relu")
            y2_done = sem("y2_done")
            x1_added = sem("x1_added")
            x1_done = sem("x1_done")
            xsum2_done = sem("xsum2_done")
            centered2 = sem("centered2")
            squared2 = sem("squared2")
            xvar2_done = sem("xvar2_done")
            std2_done = sem("std2_done")
            rs2_done = sem("rs2_done")
            normed2 = sem("normed2")
            h2_rowed = sem("h2_rowed")
            h2_stored = [sem(f"h2_stored{n}") for n in range(2)]
            h2_transposed = sem("h2_transposed")
            h2_relu = sem("h2_relu")
            root_done = sem("root_done")
            root_kept = sem("root_kept")

            loads = [(u1[:, 0, :], U1[0:D, :]), (u1[:, 1, :], U1[D:2 * D, :]), (u2[:, :], U2), (rootw[:, :], root),
                     (c1c[:, :], col(c1)), (biasc[:, :], col(bias)), (c2b[:, :], c2.partition_broadcast(P))]

            with nc.Block() as block:
                @block.sync
                def _(sp):
                    for to, frm in loads:
                        sp.dma_start(to, frm).then_inc(wts_loaded, 16)
                    sp.dma_start(xa[:, 0:2 * CH, :], x_rows[:, 0:2 * CH, :]).then_inc(x_first, 16)
                    sp.dma_start(xa[:, 2 * CH:NT, :], x_rows[:, 2 * CH:NT, :]).then_inc(x_again, 16)

                    def step(i, u):
                        k = 2 * i + u
                        sp.wait_ge(h2_rowed, k + 1)
                        sp.dma_start(h2_rows[:, bass.ds(k * CH, CH), :],
                                     hr2[:, u, :].rearrange("p (t d) -> p t d", t=CH)).then_inc(h2_stored[u], 16)
                    pairs(sp, step)
                    for u in range(2):
                        sp.wait_ge(h2_stored[u], 16 * (NCH // 2))

                @block.tensor
                def _(pe):
                    pe.wait_ge(wts_loaded, 16 * len(loads))

                    def first_layer(k):
                        after(pe, y1_relu, k)
                        for a, n in ((0, CA), (CA, CW - CA)):
                            nc.tensor.matmul(psY[:, a:a + n], u1[:, 0, :], hT[:, bass.ds(k * CW + a, n)], start=True, stop=False)
                            ins = nc.tensor.matmul(psY[:, a:a + n], u1[:, 1, :], aggT[:, bass.ds(k * CW + a, n)], start=False, stop=True)
                        ins.then_inc(y1_done, 1)

                    def second_layer(k):
                        pe.wait_ge(y1_relu, k + 1)
                        after(pe, x1_added, k)
                        for t in range(CH):
                            ins = nc.tensor.matmul(psX[:, t * P:(t + 1) * P], y1[:, t * P:(t + 1) * P], u2[:, :],
                                                   start=True, stop=True)
                        ins.then_inc(y2_done, 1)

                    def turn(k, u):
                        pe.wait_ge(normed2, k + 1)
                        after(pe, h2_relu, k)
                        for t in range(CH):
                            ins = nc.tensor.transpose(psA[:, t * P:(t + 1) * P], hn2[:, u, t, :], ident[:, :])
                        ins.then_inc(h2_transposed, 1)

                    def root_term(k):
                        pe.wait_ge(h2_relu, k + 1)
                        after(pe, root_kept, k)
                        for a, n in ((0, CA), (CA, CW - CA)):
                            ins = nc.tensor.matmul(psR[:, a:a + n], rootw[:, :], hs2[:, a:a + n], start=True, stop=True)
                        ins.then_inc(root_done, 1)

                    def step(i, u):
                        k = 2 * i + u
                        first_layer(k)
                        if there(k - 3):
                            root_term(k - 3)
                        second_layer(k)
                        if there(k - 2):
                            turn(k - 2, u)
                    pairs(pe, step, 2)
                    root_term(NCH - 3)
                    turn(NCH - 2, 0)
                    root_term(NCH - 2)
                    turn(NCH - 1, 1)
                    root_term(NCH - 1)

                @block.scalar
                def _(act):
                    act.wait_ge(wts_loaded, 16 * len(loads))
                    act.wait_ge(epsd_ready, 1)

                    def update(k):
                        act.wait_ge(y1_done, k + 1)
                        after(act, y2_done, k)
                        nc.scalar.activation(y1[:, :], psY[:, 0:CW], ACT.Relu, bias=c1c[:, 0:1]).then_inc(y1_relu, 1)

                    def square(k, u):
                        act.wait_ge(centered2, k + 1)
                        after(act, xvar2_done, k)
                        nc.scalar.activation(sq2[:, :], flat(hn2[:, u, :, :]), ACT.Square).then_inc(squared2, 1)

                    def deviation(k):
                        act.wait_ge(xvar2_done, k + 1)
                        after(act, rs2_done, k)
                        nc.scalar.activation(std2[:, :], xvar2[:, :], ACT.Sqrt, bias=epsd[:, 0:1], scale=1.0 / D).then_inc(std2_done, 1)

                    def relu(k, u, n):
                        act.wait_ge(h2_transposed, k + 1)
                        after(act, root_done, k)
                        nc.scalar.activation(hs2[:, :], psA[:, 0:CW], ACT.Relu).then_inc(h2_relu, 1)
                        after(act, h2_stored[u], 16 * n)
                        nc.scalar.activation(hr2[:, u, :], flat(hn2[:, u, :, :]), ACT.Relu).then_inc(h2_rowed, 1)

                    def keep_root(k):
                        act.wait_ge(root_done, k + 1)
                        nc.scalar.activation(aggT[:, bass.ds(k * CW, CW)], psR[:, 0:CW], ACT.Identity,
                                             bias=biasc[:, 0:1]).then_inc(root_kept, 1)

                    def step(i, u):
                        k = 2 * i + u
                        update(k)
                        if there(k - 1):
                            square(k - 1, 1 - u)
                        if there(k - 3):
                            keep_root(k - 3)
                        if there(k - 1):
                            deviation(k - 1)
                        if there(k - 2):
                            relu(k - 2, u, i - 1)
                    pairs(act, step, 2)
                    square(NCH - 1, 1)
                    keep_root(NCH - 3)
                    deviation(NCH - 1)
                    relu(NCH - 2, 0, NCH // 2 - 1)
                    keep_root(NCH - 2)
                    relu(NCH - 1, 1, NCH // 2 - 1)
                    keep_root(NCH - 1)

                @block.vector
                def _(dve):
                    nc.vector.memset(epsd[:, :], EPS).then_inc(epsd_ready, 1)
                    nc.vector.memset(aggT[:, NP:NP + W], 0.0)
                    dve.wait_ge(wts_loaded, 16 * len(loads))
                    dve.wait_ge(x_first, 16)

                    def update(k, u):
                        xc = xa[:, bass.ds(k * CH, CH), :]
                        dve.wait_ge(y2_done, k + 1)
                        nc.vector.tensor_tensor(xc, psX[:, 0:CW].rearrange("p (t d) -> p t d", t=CH), xc, ALU.add).then_inc(x1_added, 1)
                        dve.wait_ge(x1_added, k + 1)
                        nc.vector.tensor_tensor(xc, xc, c2b[:, :].unsqueeze(1).to_broadcast([P, CH, D]), ALU.add).then_inc(x1_done, 1)
                        dve.wait_ge(x1_done, k + 1)
                        dve.nop(nofuse=True)
                        nc.vector.tensor_reduce(xsum2[:, :], xc, AX.X, ALU.add).then_inc(xsum2_done, 1)
                        dve.wait_ge(xsum2_done, k + 1)
                        if there(k - 2):
                            dve.wait_ge(h2_transposed, k - 1)
                            dve.wait_ge(h2_rowed, k - 1)
                        nc.vector.scalar_tensor_tensor(out=hn2[:, u, :, :], in0=xsum2[:, :].unsqueeze(2).to_broadcast([P, CH, D]),
                                                       scalar=-1.0 / D, in1=xc, op0=ALU.mult, op1=ALU.add).then_inc(centered2, 1)

                    def scale(k, u):
                        dve.wait_ge(std2_done, k + 1)
                        nc.vector.reciprocal(rs2[:, :], std2[:, :]).then_inc(rs2_done, 1)
                        dve.wait_ge(rs2_done, k + 1)
                        nc.vector.tensor_tensor(hn2[:, u, :, :], hn2[:, u, :, :], rs2[:, :].unsqueeze(2).to_broadcast([P, CH, D]),
                                                ALU.mult).then_inc(normed2, 1)

                    def variance(k):
                        dve.wait_ge(squared2, k + 1)
                        nc.vector.tensor_reduce(xvar2[:, :], sq2[:, :].rearrange("p (t d) -> p t d", t=CH), AX.X,
                                                ALU.add).then_inc(xvar2_done, 1)

                    def step(i, u):
                        k = 2 * i + u
                        update(k, u)
                        if there(k - 1):
                            scale(k - 1, 1 - u)
                        variance(k)
                        if isinstance(k, int) and k == 1:
                            dve.wait_ge(x_again, 16)
                    pairs(dve, step)
                    scale(NCH - 1, 1)

        l1_consts = sem("l1_consts")
        l1_iota = sem("l1_iota")
        l1_idx_ready = sem("l1_idx_ready")
        l1_gathered = [sem(f"l1_gathered{n}") for n in range(GPI)]
        types_hot = sem("types_hot")
        coef_step = sem("coef_step")
        hot_ready = sem("hot_ready")
        sel_ready = sem("sel_ready")
        summed = sem("summed")
        sums_copied = sem("sums_copied")
        based = sem("based")
        l1_added = sem("l1_added")
        sum_sems = [l1_consts, l1_iota, l1_idx_ready, *l1_gathered, types_hot, coef_step, hot_ready, sel_ready, summed,
                    sums_copied, based, l1_added]

        def sum_edges(tag):
            with ExitStack() as ph:
                sb, ps = tensors(ph, tag)
                G = hT[:, 0:GPI * GT * D].rearrange("p (s j d) -> p s j d", s=GPI, j=GT)
                typ = sb("typ", [P, ET], i32)
                relc = sb("relc1", [P, ET], bf16)
                V = sb("V", [P, NB, D], fp32)
                compb = sb("compb", [P, NB, NR], fp32)
                rel_no = sb("rel_no", [P, NR], fp32)
                thot = sb("thot", [P, TPI, NR], fp32)
                tprod = sb("tprod", [P, TPI, NB, NR], fp32)
                coef = sb("coef", [P, TPI, NB], fp32)
                hot = sb("hot", [P, 2, GT, W], fp32)
                S = sb("S", [P, 2, GT, NB, W], fp32)
                A = sb("A", [P, 2, NB, W], fp32)
                idxs = sb("idxs1", [P, GPI, GT], i32)
                psA = ps("psA1", [P, 2, 512])
                psV = ps("psV1", [P, 2, 512])

                with nc.Block() as block:
                    @block.sync
                    def _(sp):
                        sp.dma_start(V[:, :, :], basis.rearrange("b i o -> i b o")).then_inc(l1_consts, 16)
                        for b in range(NB):
                            sp.dma_start(compb[:, b, :], comp_t[b, :].partition_broadcast(P)).then_inc(l1_consts, 16)
                        sp.dma_start(relc[:, :], relc_tab).then_inc(l1_consts, 16)
                        sp.dma_start(typ[:, :], type_cols).then_inc(l1_consts, 16)

                    @block.gpsimd
                    def _(pool):
                        pool.iota(rel_no[:, :], pattern=[[1, NR]], base=0, channel_multiplier=0,
                                  allow_small_or_imprecise_dtypes=True).then_inc(l1_iota, 1)

                        def step(i, s):
                            k = GPI * i + s
                            pool.wait_ge(l1_idx_ready, k + 1)
                            pool.nop(nofuse=True)
                            if there(k - GPI):
                                pool.wait_ge(summed, k - GPI + 1)
                                pool.nop(nofuse=True)
                            for j in range(GT):
                                pool.indirect_dma_start(G[:, s, j, :], None, h2_tab,
                                                        bass.IndirectOffsetOnAxis(ap=idxs[:, s, j:j + 1], axis=0)
                                                        ).then_inc(l1_gathered[s], 16)
                        sweep(pool, step)

                    @block.tensor
                    def _(pe):
                        pe.wait_ge(l1_consts, 16 * (NB + 3))

                        def sums(i, s):
                            k, b = GPI * i + s, s % 2
                            pe.wait_ge(sel_ready, k + 1)
                            if there(k - 2):
                                pe.wait_ge(sums_copied, k - 1)
                            pe.wait_ge(l1_gathered[s], 16 * GT * (i + 1))
                            for j in range(GT):
                                ins = nc.tensor.matmul(psA[:, b, 0:NB * W], G[:, s, j, :],
                                                       S[:, b, j, :, :].rearrange("p b w -> p (b w)"),
                                                       start=j == 0, stop=j == GT - 1)
                            ins.then_inc(summed, 1)

                        def bases(k, b):
                            pe.wait_ge(sums_copied, k + 1)
                            if there(k - 2):
                                pe.wait_ge(l1_added, k - 1)
                            for n in range(NB):
                                ins = nc.tensor.matmul(psV[:, b, 0:W], V[:, n, :], A[:, b, n, :], start=n == 0, stop=n == NB - 1)
                            ins.then_inc(based, 1)

                        def step(i, s):
                            k = GPI * i + s
                            sums(i, s)
                            if there(k - 1):
                                bases(k - 1, (s + 1) % 2)
                        sweep(pe, step)
                        bases(NGRP - 1, 1)

                    @block.scalar
                    def _(act):
                        def step(i, s):
                            k, b = GPI * i + s, s % 2
                            act.wait_ge(summed, k + 1)
                            if there(k - 2):
                                act.wait_ge(based, k - 1)
                            nc.scalar.activation(A[:, b, :, :].rearrange("p b w -> p (b w)"), psA[:, b, 0:NB * W],
                                                 ACT.Copy).then_inc(sums_copied, 1)
                        sweep(act, step)

                    @block.vector
                    def _(dve):
                        dve.wait_ge(l1_consts, 16 * (NB + 3))
                        dve.wait_ge(l1_iota, 1)

                        def indices(i, s):
                            k = GPI * i + s
                            if there(k - GPI):
                                dve.wait_ge(l1_gathered[s], 16 * GT * i)
                            nc.vector.tensor_copy(idxs[:, s, :], idx0[:, bass.ds(k * GT, GT)]).then_inc(l1_idx_ready, 1)

                        def coefs(i):
                            dve.nop(nofuse=True)
                            nc.vector.tensor_tensor(thot[:, :, :], typ[:, bass.ds(i * TPI, TPI)].unsqueeze(2).to_broadcast([P, TPI, NR]),
                                                    rel_no[:, :].unsqueeze(1).to_broadcast([P, TPI, NR]),
                                                    ALU.is_equal).then_inc(types_hot, 1)
                            dve.wait_ge(types_hot, i + 1)
                            for b in range(NB):
                                ins = nc.vector.tensor_tensor(tprod[:, :, b, :], thot[:, :, :],
                                                              compb[:, b, :].unsqueeze(1).to_broadcast([P, TPI, NR]), ALU.mult)
                            ins.then_inc(coef_step, 1)
                            dve.wait_ge(coef_step, 2 * i + 1)
                            nc.vector.tensor_reduce(coef[:, :, :], tprod[:, :, :, :], AX.X, ALU.add).then_inc(coef_step, 1)

                        def select(i, s):
                            k, b = GPI * i + s, s % 2
                            nc.vector.tensor_tensor(hot[:, b, :, :], lane[:, :].unsqueeze(1).to_broadcast([P, GT, W]),
                                                    relc[:, bass.ds(k * GT, GT)].unsqueeze(2).to_broadcast([P, GT, W]),
                                                    ALU.is_equal).then_inc(hot_ready, 1)
                            dve.wait_ge(hot_ready, k + 1)
                            dve.wait_ge(coef_step, 2 * i + 2)
                            if there(k - 2):
                                dve.wait_ge(summed, k - 1)
                            for j in range(GT):
                                ins = nc.vector.tensor_tensor(S[:, b, j, :, :], hot[:, b, j, :].unsqueeze(1).to_broadcast([P, NB, W]),
                                                              coef[:, s * GT + j, :].unsqueeze(2).to_broadcast([P, NB, W]), ALU.mult)
                            ins.then_inc(sel_ready, 1)

                        def add(k, b):
                            dve.wait_ge(based, k + 1)
                            after(dve, l1_added, k)
                            dve.nop(nofuse=True)
                            r0 = dve.value_load(win[0:1, bass.ds(k, 1)], min_val=0, max_val=NP)
                            to = aggT[:, bass.ds(r0, W)]
                            nc.vector.tensor_tensor(to, psV[:, b, 0:W], to, ALU.add).then_inc(l1_added, 1)

                        for s in range(AHEAD):
                            indices(0, s)

                        def step(i, s):
                            k = GPI * i + s
                            if not (isinstance(k, int) and k + AHEAD >= NGRP):
                                indices(i + (s + AHEAD) // GPI, (s + AHEAD) % GPI)
                            if s == 0:
                                coefs(i)
                            select(i, s)
                            if there(k - 2):
                                add(k - 2, s % 2)
                        sweep(dve, step)
                        add(NGRP - 2, 0)
                        add(NGRP - 1, 1)

        win_reset = sem("win_reset")
        more = passes()
        with nc.If(more > 1):
            enter()
            clear(mark_sems)
            with nc.Block() as block:
                @block.sync
                def _(sp):
                    sp.dma_start(win[:, :], row(first)).then_inc(win_reset, 16)

                @block.vector
                def _(dve):
                    dve.wait_ge(win_reset, 16)
                    nc.vector.tensor_scalar(win[0:1, :], win[0:1, :], -float(W), None, ALU.add).then_inc(win_moved, 1)
                    nc.vector.memset(shift[:, :], float(W)).then_inc(win_moved, 1)
            move_windows("_b")
        nc.end_ifs()
        sum_edges("")
        more = passes()
        with nc.If(more > 1):
            enter()
            with nc.Fori(1, more):
                clear(mark_sems + sum_sems)
                move_windows("_c")
                sum_edges("_c")
        nc.end_ifs()

        with ExitStack() as ph:
            sb, ps = tensors(ph)
            ra = sb("ra", [P, 2, CW], fp32)
            psT = ps("psT", [P, 2, 1024])
            ra_done = sem("ra_done")
            ra_transposed = sem("ra_transposed")
            x2_done = sem("x2_done")
            out_stored = sem("out_stored")

            with nc.Block() as block:
                @block.scalar
                def _(act):
                    def step(i, u):
                        k = 2 * i + u
                        if there(k - 2):
                            act.wait_ge(ra_transposed, k - 1)
                        nc.scalar.activation(ra[:, u, :], aggT[:, bass.ds(k * CW, CW)], ACT.Relu).then_inc(ra_done, 1)
                    pairs(act, step)

                @block.tensor
                def _(pe):
                    def step(i, u):
                        k = 2 * i + u
                        pe.wait_ge(ra_done, k + 1)
                        if there(k - 2):
                            pe.wait_ge(x2_done, k - 1)
                        for t in range(CH):
                            ins = nc.tensor.transpose(psT[:, u, t * P:(t + 1) * P], ra[:, u, t * P:(t + 1) * P], ident[:, :])
                        ins.then_inc(ra_transposed, 1)
                    pairs(pe, step)

                @block.vector
                def _(dve):
                    def step(i, u):
                        k = 2 * i + u
                        dve.wait_ge(ra_transposed, k + 1)
                        xc = xa[:, bass.ds(k * CH, CH), :]
                        nc.vector.tensor_tensor(xc, psT[:, u, 0:CW].rearrange("p (t d) -> p t d", t=CH), xc, ALU.add).then_inc(x2_done, 1)
                    pairs(dve, step)

                @block.sync
                def _(sp):
                    def step(i, u):
                        k = 2 * i + u
                        sp.wait_ge(x2_done, k + 1)
                        sp.dma_start(out_rows[:, bass.ds(k * CH, CH), :], xa[:, bass.ds(k * CH, CH), :]).then_inc(out_stored, 16)
                    pairs(sp, step)
                    sp.wait_ge(out_stored, 16 * NCH)


_INS = ['x', 'dst', 'first', 'last', 'src_cols', 'dst_cols', 'next_cols', 'type_cols', 'w', 'W1', 'b1', 'W2', 'b2', 'U1', 'c1',
        'U2', 'c2', 'basis', 'comp_t', 'root', 'bias']


def kernel(x, src, dst, edge_type_8, edge_weight, L0_gnn_W1, L0_gnn_b1, L0_gnn_W2, L0_gnn_b2, L0_gnn_U1, L0_gnn_c1,
           L0_gnn_U2, L0_gnn_c2, L1_gnn_weight, L1_gnn_w_comp, L1_gnn_root_weight, L1_gnn_bias):
    import numpy as np
    import concourse.bacc as bacc
    from concourse.bass_utils import run_bass_kernel_spmd as run

    x, src, dst, kind, w = (np.asarray(a) for a in (x, src, dst, edge_type_8, edge_weight))
    n, d = x.shape
    e = src.shape[0]
    n_pad = -(-n // (14 * P)) * 14 * P
    e_pad = -(-e // (TPI * P)) * TPI * P
    assert n < n_pad

    def columns(v):
        return np.ascontiguousarray(v.reshape(-1, P).T)

    def padded(v, fill):
        return np.pad(v, (0, e_pad - e), constant_values=fill)

    dst_pad = padded(dst, n)
    ins = {
        'x': np.pad(x, ((0, n_pad - n), (0, 0))), 'dst': np.pad(dst_pad, (1, 0), constant_values=-1),
        'first': dst_pad[::GE], 'last': dst_pad[GE - 1::GE], 'src_cols': columns(padded(src, 0)), 'dst_cols': columns(dst_pad),
        'next_cols': columns(np.pad(dst_pad, (0, 1), constant_values=-1)[1:]), 'type_cols': columns(padded(kind, 0)),
        'w': padded(w, 0),
        'W1': L0_gnn_W1, 'b1': L0_gnn_b1, 'W2': L0_gnn_W2, 'b2': L0_gnn_b2, 'U1': L0_gnn_U1, 'c1': L0_gnn_c1,
        'U2': L0_gnn_U2, 'c2': L0_gnn_c2, 'basis': L1_gnn_weight, 'comp_t': np.asarray(L1_gnn_w_comp).T,
        'root': L1_gnn_root_weight, 'bias': L1_gnn_bias}
    nc = bacc.Bacc("TRN2", target_bir_lowering=False, num_devices=1)
    arrays, args = {}, []
    for name in _INS:
        a = np.ascontiguousarray(ins[name])
        arrays[f"in_{name}"] = a
        args.append(nc.dram_tensor(f"in_{name}", a.shape, mybir.dt.from_np(a.dtype), kind="ExternalInput").ap())
    args.append(nc.dram_tensor("out_x", (n_pad, d), mybir.dt.float32, kind="ExternalOutput").ap())
    gnn(nc, *args, n)
    r = run(nc, [arrays], core_ids=[0])
    return r.results[0]["out_x"][:n]
```
